# Optimizing a Trainium2 kernel written in Bass

```python
import numpy as np
import jax
import jax.numpy as jnp

def _softmax(x, axis=-1):
    return jax.nn.softmax(x, axis=axis)

def _gelu(x):
    return jax.nn.gelu(x, approximate=True)

def _silu(x):
    return jax.nn.silu(x)

def _sigmoid(x):
    return jax.nn.sigmoid(x)

def _layernorm(x, axis=-1, eps=1e-05):
    m = jnp.mean(x, axis=axis, keepdims=True)
    v = jnp.var(x, axis=axis, keepdims=True)
    return (x - m) / jnp.sqrt(v + eps)

def _scatter_add(tgt, idx, src, axis=0):
    return tgt.at[idx].add(src)

def _segment_sum(src, seg, n):
    return jax.ops.segment_sum(src, seg, n)
kernel_name = 'mk_seq_postln_d1_jaxref_r4_66ff6c'

def setup_inputs(seed: int=0):
    np.random.seed(seed)
    _w = jnp.asarray

    def _L0_attn_setup():
        import jax, jax.numpy as jnp
        import numpy as np
        HID = 512
        H = 16
        QLR = 384
        KVLR = 128
        DN = 128
        DR = 64
        DV = 128
        DQ = DN + DR
        B = 2
        S = 512
        THETA = 10000.0
        EPS = 1e-06

        def rms_norm(x, w, eps=EPS):
            x32 = x.astype(jnp.float32)
            var = jnp.mean(x32 * x32, axis=-1, keepdims=True)
            return (w * (x32 * jax.lax.rsqrt(var + eps))).astype(x.dtype)

        def rotate_half(x):
            x1, x2 = jnp.split(x, 2, axis=-1)
            return jnp.concatenate((-x2, x1), axis=-1)

        def rope_tables(seq_len, dim, base=THETA):
            inv_freq = 1.0 / base ** (jnp.arange(0, dim, 2, dtype=jnp.float32) / dim)
            t = jnp.arange(seq_len, dtype=jnp.float32)
            freqs = jnp.outer(t, inv_freq)
            emb = jnp.concatenate((freqs, freqs), -1)
            return (jnp.cos(emb), jnp.sin(emb))
        key = jax.random.key(seed)
        ks = jax.random.split(key, 8)
        sd = lambda fan_in: 1.0 / np.sqrt(fan_in)
        return {'hidden_states': jax.random.normal(ks[0], (B, S, HID), jnp.float32), 'w_qa': jax.random.normal(ks[1], (QLR, HID), jnp.float32) * sd(HID), 'q_a_ln_w': jnp.ones((QLR,), jnp.float32), 'w_qb': jax.random.normal(ks[2], (H * DQ, QLR), jnp.float32) * sd(QLR), 'w_kva': jax.random.normal(ks[3], (KVLR + DR, HID), jnp.float32) * sd(HID), 'kv_a_ln_w': jnp.ones((KVLR,), jnp.float32), 'w_kvb': jax.random.normal(ks[4], (H * (DN + DV), KVLR), jnp.float32) * sd(KVLR), 'w_o': jax.random.normal(ks[5], (HID, H * DV), jnp.float32) * sd(H * DV)}
    _L0_attn_in = _L0_attn_setup()

    def _L0_ffn_setup():
        import jax, jax.numpy as jnp
        import numpy as np
        key = jax.random.key(seed)
        k1, k2, k3, k4 = jax.random.split(key, 4)
        B, S, D_IN, D_OUT = (4, 1024, 512, 512)
        x = jax.random.normal(k1, (B, S, D_IN), dtype=jnp.float32)
        weight = jax.random.normal(k2, (D_OUT, D_IN), dtype=jnp.float32) * 0.02
        scale_weight = jax.random.uniform(k3, (D_OUT,), dtype=jnp.float32, minval=0.5, maxval=1.5)
        bias = jax.random.normal(k4, (D_OUT,), dtype=jnp.float32) * 0.02
        return {'x': x, 'weight': weight, 'scale_weight': scale_weight, 'bias': bias}
    _L0_ffn_in = _L0_ffn_setup()
    _d = {'L0_attn_hidden_states': _L0_attn_in['hidden_states'], 'L0_attn_w_qa': _L0_attn_in['w_qa'], 'L0_attn_q_a_ln_w': _L0_attn_in['q_a_ln_w'], 'L0_attn_w_qb': _L0_attn_in['w_qb'], 'L0_attn_w_kva': _L0_attn_in['w_kva'], 'L0_attn_kv_a_ln_w': _L0_attn_in['kv_a_ln_w'], 'L0_attn_w_kvb': _L0_attn_in['w_kvb'], 'L0_attn_w_o': _L0_attn_in['w_o'], 'L0_ffn_weight': _L0_ffn_in['weight'], 'L0_ffn_scale_weight': _L0_ffn_in['scale_weight'], 'L0_ffn_bias': _L0_ffn_in['bias']}
    _x0 = _d['L0_attn_hidden_states']
    _d['L0_attn_hidden_states'] = jax.random.normal(jax.random.fold_in(jax.random.key(seed), 1), (1, 2048, 512), dtype=_x0.dtype)
    del _x0
    return _d

def reference(L0_attn_hidden_states, L0_attn_w_qa, L0_attn_q_a_ln_w, L0_attn_w_qb, L0_attn_w_kva, L0_attn_kv_a_ln_w, L0_attn_w_kvb, L0_attn_w_o, L0_ffn_weight, L0_ffn_scale_weight, L0_ffn_bias):

    def _L0_attn_ref(hidden_states, w_qa, q_a_ln_w, w_qb, w_kva, kv_a_ln_w, w_kvb, w_o):
        import jax, jax.numpy as jnp
        import numpy as np
        HID = 512
        H = 16
        QLR = 384
        KVLR = 128
        DN = 128
        DR = 64
        DV = 128
        DQ = DN + DR
        B = 2
        S = 512
        THETA = 10000.0
        EPS = 1e-06

        def rms_norm(x, w, eps=EPS):
            x32 = x.astype(jnp.float32)
            var = jnp.mean(x32 * x32, axis=-1, keepdims=True)
            return (w * (x32 * jax.lax.rsqrt(var + eps))).astype(x.dtype)

        def rotate_half(x):
            x1, x2 = jnp.split(x, 2, axis=-1)
            return jnp.concatenate((-x2, x1), axis=-1)

        def rope_tables(seq_len, dim, base=THETA):
            inv_freq = 1.0 / base ** (jnp.arange(0, dim, 2, dtype=jnp.float32) / dim)
            t = jnp.arange(seq_len, dtype=jnp.float32)
            freqs = jnp.outer(t, inv_freq)
            emb = jnp.concatenate((freqs, freqs), -1)
            return (jnp.cos(emb), jnp.sin(emb))
        b, s, _ = hidden_states.shape
        scale = DQ ** (-0.5)
        cos, sin = rope_tables(s, DR)
        cq = rms_norm(hidden_states @ w_qa.T, q_a_ln_w)
        q = (cq @ w_qb.T).reshape(b, s, H, DQ).transpose(0, 2, 1, 3)
        q_nope, q_pe = (q[..., :DN], q[..., DN:])
        q_pe = q_pe * cos + rotate_half(q_pe) * sin
        ckv = hidden_states @ w_kva.T
        k_pe = ckv[..., KVLR:].reshape(b, s, 1, DR).transpose(0, 2, 1, 3)
        k_pe = k_pe * cos + rotate_half(k_pe) * sin
        ckv_l = rms_norm(ckv[..., :KVLR], kv_a_ln_w)
        kv = (ckv_l @ w_kvb.T).reshape(b, s, H, DN + DV).transpose(0, 2, 1, 3)
        k_nope, v = (kv[..., :DN], kv[..., DN:])
        q_full = jnp.concatenate([q_nope, q_pe], axis=-1)
        k_full = jnp.concatenate([k_nope, jnp.broadcast_to(k_pe, (b, H, s, DR))], axis=-1)
        scores = jnp.einsum('bhqd,bhkd->bhqk', q_full, k_full) * scale
        causal = jnp.triu(jnp.ones((s, s), dtype=bool), k=1)
        scores = jnp.where(causal, -jnp.inf, scores)
        attn = jax.nn.softmax(scores.astype(jnp.float32), axis=-1).astype(q_full.dtype)
        out = jnp.einsum('bhqk,bhkd->bhqd', attn, v)
        out = out.transpose(0, 2, 1, 3).reshape(b, s, H * DV)
        return out @ w_o.T

    def _L0_ffn_ref(x, weight, scale_weight, bias):
        import jax, jax.numpy as jnp
        import numpy as np
        w = weight * scale_weight[:, None]
        out = jnp.einsum('bsi,oi->bso', x, w) + bias
        return out
    x = L0_attn_hidden_states
    x = _layernorm(x + _L0_attn_ref(x, L0_attn_w_qa, L0_attn_q_a_ln_w, L0_attn_w_qb, L0_attn_w_kva, L0_attn_kv_a_ln_w, L0_attn_w_kvb, L0_attn_w_o), axis=-1)
    x = _layernorm(x + _L0_ffn_ref(x, L0_ffn_weight, L0_ffn_scale_weight, L0_ffn_bias), axis=-1)
    return x

_drawn_inputs = setup_inputs


def setup_inputs(seed=0):
    import zlib

    import numpy as np

    out = dict(_drawn_inputs(seed))
    spreads = {'L0_attn_q_a_ln_w': (1.0, 0.6), 'L0_attn_kv_a_ln_w': (1.0, 0.2)}
    factors = {'L0_ffn_bias': 3.389}
    for name, (base, spread) in spreads.items():
        noise = np.random.default_rng([zlib.crc32(name.encode()), seed]).standard_normal(out[name].shape)
        drawn = base * np.exp(spread * noise) if base else spread * noise
        out[name] = jnp.asarray(drawn.astype(out[name].dtype))
    for name, factor in factors.items():
        out[name] = (out[name] * factor).astype(out[name].dtype)
    return out
```

```python
from contextlib import ExitStack

import numpy as np

import concourse.bass as bass
from concourse import mybir

F32 = mybir.dt.float32
F32R = mybir.dt.float32r
BF16 = mybir.dt.bfloat16
ALU = mybir.AluOpType
ACT = mybir.ActivationFunctionType
AX = mybir.AxisListType

P = 128
S = 2048
HID = 512
H = 16
QLR = 384
C = 128
DN, DR, DV = 128, 64, 128
DQ = DN + DR
HALF = DR // 2
SCALE = DQ ** -0.5
RMS_EPS, LN_EPS = 1e-6, 1e-5
MASKED = -1e38

NT = S // P
NCH = NT // 4
G = 4
HG = H // G
KR = QLR // P
KH = HID // P
WCOL = HG * C + HG * DR
PAIRS = HG // 2


def stored(view):
    return view.bitcast(F32)


def words(buffer):
    return stored(buffer[:, :, :, :].rearrange("p a k n -> p (a k n)"))


class Memory:

    def __init__(self, nc, ctx):
        def sb(name, shape, dt=F32):
            return ctx.enter_context(nc.sbuf_tensor(name, shape, dt))

        self.bank = [ctx.enter_context(nc.psum_tensor(f"bank{n}", [P, 512], F32)) for n in range(4, 8)]
        self.rows = ctx.enter_context(nc.psum_tensor("rows", [P, 4 * 512], F32))
        self.bank = [self.rows[:, 512 * n:512 * n + 512] for n in range(4)] + [b[:, :] for b in self.bank]

        self.key_c = sb("key_c", [P, 2, S], F32R)
        self.key_pe = sb("key_pe", [P, 2, S], F32R)
        self.val = sb("val", [P, 2, NT, C], F32R)
        self.cq = sb("cq", [P, 2, KR, 512], F32R)
        self.wq = sb("wq", [P, 2, KR, WCOL], F32R)
        self.wo = sb("wo", [P, 2, HG, HID], F32R)
        self.ident = sb("ident", [P, P])
        self.ident16 = sb("ident16", [P, P], BF16)
        self.mask16 = sb("mask16", [P, P], BF16)
        self.cos = sb("cos", [P, NT, HALF])
        self.sin = sb("sin", [P, NT, HALF])
        self.small = sb("small", [P, 64])
        self.pool = sb("pool", [P, HG * (NT - 1) * P + HG * NT * P])

        self.cq_dram = nc.dram_tensor("cq_dram", (NCH, P, 2 * KR * 512), F32, kind="Internal").ap()
        self.wq_dram = nc.dram_tensor("wq_dram", (G, P, 2 * KR * WCOL), F32, kind="Internal").ap()
        self.wo_dram = nc.dram_tensor("wo_dram", (G, P, 2 * HG * HID), F32, kind="Internal").ap()
        self.y_stored = ctx.enter_context(nc.semaphore("y_stored"))
        self.y_dram = nc.dram_tensor("y_dram", (NT, P, HID), F32, kind="Internal").ap()


def weights_phase(nc, m, x, w_qb, w_kvb, w_o, q_ln, kv_ln, ident_in, mask_in, cos_in, sin_in):
    with ExitStack() as ctx:
        def sem(name):
            return ctx.enter_context(nc.semaphore(name))

        at = 0

        def stage(n):
            nonlocal at
            at += n
            return m.pool[:, at - n:at]

        nope = stage(HG * QLR).rearrange("p (h r) -> p h r", h=HG)
        pe = stage(PAIRS * QLR).rearrange("p (a r) -> p a r", a=PAIRS)
        kv = stage(HG * 2 * C).rearrange("p (h k c) -> p h k c", h=HG, k=2)
        wo_rows = stage(KH * HG * DV).rearrange("p (o d) -> p o d", o=KH)
        wo_t = stage(HG * HID).rearrange("p (h o) -> p h o", h=HG)
        mask = stage(P)
        q_w = m.small[:, 0:KR]
        kv_w = m.small[:, 4:5]

        const_loaded = sem("const_loaded")
        consts_cast = sem("consts_cast")
        raw_loaded = sem("raw_loaded")
        psum_ready = sem("psum_ready")
        wot_copied = sem("wot_copied")
        hi_done = sem("hi_done")
        lo_done = sem("lo_done")
        split_stored = sem("split_stored")

        NOPE, PET, WOT, WOV = 0, KR, KR + 2, KR + 2 + HG
        FILLS = WOV + HG
        SPLITS = KR + KR + HG

        wqb_v = w_qb.rearrange("(g h q) r -> g q h r", g=G, h=HG)
        wpe_v = w_qb.rearrange("(g a e q) r -> g e q a r", g=G, a=PAIRS, e=2)
        kvb_v = w_kvb.rearrange("(g h k d) c -> g d (h k) c", g=G, h=HG, k=2)
        wo_v = w_o.rearrange("(o p) (g n) -> g p o n", p=P, g=G)
        LOADS = 5

        block = ctx.enter_context(nc.Block())

        @block.sync
        def _(sp):
            sp.dma_start(m.ident[:, :], ident_in).then_inc(const_loaded, 16)
            sp.dma_start(mask, mask_in).then_inc(const_loaded, 16)
            sp.dma_start(q_w, q_ln.rearrange("(k p) -> p k", p=P),
                         allow_slow_non_contiguous=True).then_inc(const_loaded, 16)
            sp.dma_start(kv_w, kv_ln.rearrange("(k p) -> p k", p=P),
                         allow_slow_non_contiguous=True).then_inc(const_loaded, 16)
            sp.dma_start(m.cos[:, :, :], cos_in.rearrange("(t p) d -> p t d", p=P)).then_inc(const_loaded, 16)
            sp.dma_start(m.sin[:, :, :], sin_in.rearrange("(t p) d -> p t d", p=P)).then_inc(const_loaded, 16)
            sp.dma_start(m.y_dram.rearrange("t p d -> (t p) d"), x).then_inc(m.y_stored, 16)

        @block.gpsimd
        def _(pool):
            def load(g):
                pool.dma_start(nope, wqb_v[g, 0:DN]).then_inc(raw_loaded, 16)
                for e in range(2):
                    pool.dma_start(pe[DR * e:DR * e + DR], wpe_v[g, e, DN:DQ]).then_inc(raw_loaded, 16)
                pool.dma_start(kv.rearrange("p h k c -> p (h k) c"), kvb_v[g]).then_inc(raw_loaded, 16)
                pool.dma_start(wo_rows, wo_v[g]).then_inc(raw_loaded, 16)

            load(0)

            def store(g):
                pool.wait_ge(lo_done, g * SPLITS + SPLITS)
                pool.dma_start(m.wq_dram[g], words(m.wq)).then_inc(split_stored, 16)
                pool.dma_start(m.wo_dram[g], words(m.wo)).then_inc(split_stored, 16)

            with pool.Fori(0, G - 1) as g:
                pool.wait_ge(psum_ready, g * FILLS + FILLS)
                load(g + 1)
                store(g)
            store(G - 1)
            pool.wait_ge(split_stored, 32 * G)

        @block.tensor
        def _(pe_eng):
            pe_eng.wait_ge(const_loaded, 16 * 6)
            with pe_eng.Fori(0, G) as g:
                pe_eng.wait_ge(raw_loaded, g * (16 * LOADS) + 16 * LOADS)
                for k in range(KR):
                    for h in range(HG):
                        mm = pe_eng.matmul(m.bank[k][:, h * C:h * C + C], nope[:, h, k * P:k * P + P],
                                           kv[:, h, 0, :], start=True, stop=True)
                    mm.then_inc(psum_ready, 1)
                for k in range(KR):
                    for a in range(PAIRS):
                        o = (k % 2) * 256 + a * P
                        mm = pe_eng.transpose(m.bank[3 + k // 2][:, o:o + P], pe[:, a, k * P:k * P + P],
                                              m.ident[:, :])
                    if k % 2 or k == KR - 1:
                        mm.then_inc(psum_ready, 1)
                for h in range(HG):
                    if h >= 2:
                        pe_eng.wait_ge(wot_copied, g * HG + h - 1)
                    for o in range(KH):
                        mm = pe_eng.transpose(m.bank[5 + h % 2][:, o * P:o * P + P],
                                              wo_rows[:, o, h * DV:h * DV + DV], m.ident[:, :])
                    mm.then_inc(psum_ready, 1)
                for h in range(HG):
                    pe_eng.wait_ge(wot_copied, g * HG + h + 1)
                    if h >= 1:
                        pe_eng.wait_ge(lo_done, g * SPLITS + 2 * KR + h)
                    mm = pe_eng.matmul(m.bank[7], kv[:, h, 1, :], wo_t[:, h, :], start=True, stop=True)
                    mm.then_inc(psum_ready, 1)
                pe_eng.wait_ge(lo_done, g * SPLITS + SPLITS)

        def banks_of_splits():
            for k in range(KR):
                yield m.bank[k], lambda a, k=k: m.wq[:, a, k, 0:HG * C], q_w[:, k:k + 1], NOPE + k
            for k in range(KR):
                o = (k % 2) * 256
                yield (m.bank[3 + k // 2][:, o:o + 256], lambda a, k=k: m.wq[:, a, k, HG * C:WCOL],
                       q_w[:, k:k + 1], PET + k // 2)
            for h in range(HG):
                yield m.bank[7], lambda a, h=h: m.wo[:, a, h, :], kv_w, WOV + h

        @block.scalar
        def _(act):
            act.wait_ge(consts_cast, 3)
            with act.Fori(0, G) as g:
                for n, (src, dst, scale, fill) in enumerate(banks_of_splits()):
                    if n == 2 * KR:
                        for h in range(HG):
                            act.wait_ge(psum_ready, g * FILLS + WOT + h + 1)
                            nc.scalar.copy(wo_t[:, h, :], m.bank[5 + h % 2]).then_inc(wot_copied, 1)
                    act.wait_ge(psum_ready, g * FILLS + fill + 1)
                    nc.scalar.activation(dst(0), src, ACT.Copy, scale=scale).then_inc(hi_done, 1)
                act.wait_ge(split_stored, g * 32 + 32)

        @block.vector
        def _(dve):
            dve.wait_ge(const_loaded, 16 * 6)
            nc.vector.tensor_copy(m.ident16[:, :], m.ident[:, :]).then_inc(consts_cast, 1)
            nc.vector.tensor_copy(m.mask16[:, :], mask).then_inc(consts_cast, 1)
            nc.vector.tensor_scalar(q_w, q_w, SCALE, None, ALU.mult).then_inc(consts_cast, 1)
            dve.wait_ge(consts_cast, 3)
            with dve.Fori(0, G) as g:
                for n, (src, dst, scale, fill) in enumerate(banks_of_splits()):
                    dve.wait_ge(hi_done, g * SPLITS + n + (2 if n == KR else 1))
                    nc.vector.scalar_tensor_tensor(out=dst(1), in0=src, scalar=scale, in1=stored(dst(0)),
                                                   op0=ALU.mult, op1=ALU.subtract).then_inc(lo_done, 1)
                dve.wait_ge(split_stored, g * 32 + 32)


def tokens_phase(nc, m, x, w_qa, w_kva):
    with ExitStack() as ctx:
        def sem(name):
            return ctx.enter_context(nc.semaphore(name))

        at = 0

        def stage(n):
            nonlocal at
            at += n
            return m.pool[:, at - n:at]

        WA = QLR + C + DR
        wa_rows = stage(4 * HID).rearrange("p (o i) -> p o i", o=4)
        wa_tail = stage(HID)
        wa_t = stage(KH * WA).rearrange("p (k n) -> p k n", k=KH)
        x_in = stage(4 * HID).rearrange("p (t i) -> p t i", t=4)
        x_t = [stage(HID) for _ in range(2)]
        squares = stage(QLR + C)
        cq_n = [stage(QLR) for _ in range(2)]
        c_n = [stage(C) for _ in range(2)]
        k_rot = [stage(P) for _ in range(2)]
        t_cos = stage(DR)
        t_sin = stage(DR)
        kv_w = m.small[:, 4:5]
        sums = m.small[:, 8:12]
        devs = m.small[:, 12:16]
        rstd = m.small[:, 16:20]

        wa_loaded = sem("wa_loaded")
        wa_turned = sem("wa_turned")
        wa_copied = sem("wa_copied")
        x_loaded = sem("x_loaded")
        x_turned = sem("x_turned")
        xt_copied = sem("xt_copied")
        proj_ready = sem("proj_ready")
        squared = sem("squared")
        mean_done = sem("mean_done")
        root_done = sem("root_done")
        rstd_done = sem("rstd_done")
        cqn_done = sem("cqn_done")
        cn_done = sem("cn_done")
        val_hi = sem("val_hi")
        rope_parts = sem("rope_parts")
        krot_done = sem("krot_done")
        turned = sem("turned")
        hi_done = sem("hi_done_t")
        lo_done = sem("lo_done_t")
        cq_stored = sem("cq_stored")

        block = ctx.enter_context(nc.Block())
        x_v = x.rearrange("(c t p) i -> c p t i", t=4, p=P)

        @block.sync
        def _(sp):
            sp.dma_start(wa_rows[:, 0:3, :], w_qa.rearrange("(o p) i -> p o i", p=P)).then_inc(wa_loaded, 16)
            sp.dma_start(wa_rows[:, 3, :], w_kva[0:C]).then_inc(wa_loaded, 16)
            sp.dma_start(wa_tail[0:DR], w_kva[C:C + DR]).then_inc(wa_loaded, 16)

        @block.gpsimd
        def _(pool):
            pool.dma_start(x_in, x_v[0]).then_inc(x_loaded, 16)

            def store(c):
                pool.wait_ge(lo_done, c * (KR + 2) + KR)
                pool.dma_start(m.cq_dram[c], words(m.cq)).then_inc(cq_stored, 16)

            with pool.Fori(0, NCH - 1) as c:
                pool.wait_ge(x_turned, c * 4 + 4)
                pool.dma_start(x_in, x_v[c + 1]).then_inc(x_loaded, 16)
                store(c)
            store(NCH - 1)
            pool.wait_ge(cq_stored, 16 * NCH)

        @block.tensor
        def _(pe):
            pe.wait_ge(wa_loaded, 48)
            for k in range(KH):
                for o in range(4):
                    mm = pe.transpose(m.bank[k][:, o * P:o * P + P], wa_rows[:, o, k * P:k * P + P],
                                      m.ident[:, :])
            for k in range(KH):
                mm = pe.transpose(m.bank[4][:, k * DR:k * DR + DR], wa_tail[0:DR, k * P:k * P + P],
                                  m.ident[0:DR, 0:DR])
            mm.then_inc(wa_turned, 1)
            pe.wait_ge(wa_copied, KH + 1)
            with pe.Fori(0, NCH) as c:
                pe.wait_ge(x_loaded, c * 16 + 16)

                def turn_results(t):
                    for n in range(KR):
                        if n == 0:
                            pe.wait_ge(cqn_done, c * 4 + t + 1)
                        pe.transpose(m.bank[3 + n][:, t * P:t * P + P], cq_n[t % 2][:, n * P:n * P + P],
                                     m.ident[:, :])
                    pe.wait_ge(cn_done, c * 4 + t + 1)
                    pe.transpose(m.bank[6][:, t * P:t * P + P], c_n[t % 2], m.ident[:, :])
                    pe.wait_ge(krot_done, c * 8 + 2 * t + 2)
                    pe.transpose(m.bank[7][:, t * P:t * P + P], k_rot[t % 2], m.ident[:, :]).then_inc(turned, 1)

                for t in range(4):
                    if t:
                        pe.wait_ge(xt_copied, c * 4 + t)
                    for k in range(KH):
                        mm = pe.transpose(m.bank[0][:, k * P:k * P + P], x_in[:, t, k * P:k * P + P],
                                          m.ident[:, :])
                    mm.then_inc(x_turned, 1)
                    pe.wait_ge(xt_copied, c * 4 + t + 1)
                    if t:
                        pe.wait_ge(cqn_done, c * 4 + t)
                        pe.wait_ge(cn_done, c * 4 + t)
                        pe.wait_ge(rope_parts, c * 12 + 3 * t)
                    for k in range(KH):
                        mm = pe.matmul(m.bank[1], x_t[t % 2][:, k * P:k * P + P], wa_t[:, k, 0:QLR + C],
                                       start=(k == 0), stop=(k == KH - 1))
                    for k in range(KH):
                        mm = pe.matmul(m.bank[2][:, 0:DR], x_t[t % 2][:, k * P:k * P + P],
                                       wa_t[:, k, QLR + C:WA], start=(k == 0), stop=(k == KH - 1))
                    mm.then_inc(proj_ready, 1)
                    if t:
                        turn_results(t - 1)
                turn_results(3)
                pe.wait_ge(lo_done, c * (KR + 2) + KR + 2)

        def chunk_splits(c):
            for k in range(KR):
                yield m.bank[3 + k], lambda a, k=k: m.cq[:, a, k, :], None
            yield m.bank[6], lambda a: m.key_c[:, a, bass.ds(c * 512, 512)], kv_w
            yield m.bank[7], lambda a: m.key_pe[:, a, bass.ds(c * 512, 512)], None

        @block.scalar
        def _(act):
            act.wait_ge(wa_turned, 1)
            for k in range(KH):
                nc.scalar.copy(wa_t[:, k, 0:QLR + C], m.bank[k]).then_inc(wa_copied, 1)
            nc.scalar.copy(wa_t[:, :, QLR + C:WA], m.bank[4][:, 0:KH * DR].rearrange("p (k n) -> p k n", k=KH)
                           ).then_inc(wa_copied, 1)
            with act.Fori(0, NCH) as c:
                for t in range(4):
                    b = t % 2
                    act.wait_ge(x_turned, c * 4 + t + 1)
                    nc.scalar.copy(x_t[b], m.bank[0]).then_inc(xt_copied, 1)
                    act.wait_ge(proj_ready, c * 4 + t + 1)
                    nc.scalar.activation(squares[:, 0:QLR], m.bank[1][:, 0:QLR], ACT.Square,
                                         accum_out=sums[:, 2 * b:2 * b + 1]).then_inc(squared, 1)
                    nc.scalar.activation(squares[:, QLR:QLR + C], m.bank[1][:, QLR:QLR + C], ACT.Square,
                                         accum_out=sums[:, 2 * b + 1:2 * b + 2]).then_inc(squared, 1)
                    act.wait_ge(mean_done, c * 8 + 2 * t + 2)
                    nc.scalar.activation(devs[:, 2 * b:2 * b + 2], devs[:, 2 * b:2 * b + 2], ACT.Sqrt
                                         ).then_inc(root_done, 1)
                    act.wait_ge(rstd_done, c * 4 + t + 1)
                    nc.scalar.activation(cq_n[b], m.bank[1][:, 0:QLR], ACT.Copy,
                                         scale=rstd[:, 2 * b:2 * b + 1]).then_inc(cqn_done, 1)
                act.wait_ge(turned, c * 4 + 4)
                for src, dst, scale in chunk_splits(c):
                    if scale is None:
                        nc.scalar.copy(dst(0), src).then_inc(hi_done, 1)
                    else:
                        nc.scalar.activation(dst(0), src, ACT.Copy, scale=scale).then_inc(hi_done, 1)
                act.wait_ge(cq_stored, c * 16 + 16)

        @block.vector
        def _(dve):
            with dve.Fori(0, NCH) as c:
                for t in range(4):
                    b = t % 2
                    tile = c * 4 + t
                    dve.wait_ge(squared, c * 8 + 2 * t + 2)
                    nc.vector.tensor_scalar(devs[:, 2 * b:2 * b + 1], sums[:, 2 * b:2 * b + 1], 1.0 / QLR,
                                            RMS_EPS, ALU.mult, ALU.add).then_inc(mean_done, 1)
                    nc.vector.tensor_scalar(devs[:, 2 * b + 1:2 * b + 2], sums[:, 2 * b + 1:2 * b + 2], 1.0 / C,
                                            RMS_EPS, ALU.mult, ALU.add).then_inc(mean_done, 1)
                    kp = m.bank[2][:, 0:DR].rearrange("p (a d) -> p a d", a=2)
                    cos_t = m.cos[:, bass.ds(tile, 1), :].broadcast_to([P, 2, HALF])
                    sin_t = m.sin[:, bass.ds(tile, 1), :]
                    tc = t_cos.rearrange("p (a d) -> p a d", a=2)
                    ts = t_sin.rearrange("p (a d) -> p a d", a=2)
                    nc.vector.tensor_tensor(tc, kp, cos_t, ALU.mult).then_inc(rope_parts, 1)
                    nc.vector.tensor_tensor(ts[:, 0:1], kp[:, 1:2], sin_t, ALU.mult).then_inc(rope_parts, 1)
                    nc.vector.tensor_tensor(ts[:, 1:2], kp[:, 0:1], sin_t, ALU.mult).then_inc(rope_parts, 1)
                    dve.wait_ge(rope_parts, c * 12 + 3 * t + 3)
                    kr = k_rot[b].rearrange("p (r a d) -> p r a d", r=2, a=2)
                    for a, op in ((0, ALU.subtract), (1, ALU.add)):
                        nc.vector.tensor_tensor(
                            kr[:, :, a, :], tc[:, a:a + 1, :].broadcast_to([P, 2, HALF]),
                            ts[:, a:a + 1, :].broadcast_to([P, 2, HALF]), op).then_inc(krot_done, 1)
                    dve.wait_ge(root_done, c * 4 + t + 1)
                    nc.vector.reciprocal(rstd[:, 2 * b:2 * b + 2], devs[:, 2 * b:2 * b + 2]).then_inc(rstd_done, 1)
                    dve.wait_ge(cqn_done, c * 4 + t + 1)
                    nc.vector.tensor_scalar(c_n[b], m.bank[1][:, QLR:QLR + C], rstd[:, 2 * b + 1:2 * b + 2],
                                            None, ALU.mult).then_inc(cn_done, 1)
                    dve.wait_ge(cn_done, c * 4 + t + 1)
                    v_hi = m.val[:, 0, bass.ds(tile, 1), :]
                    v_lo = m.val[:, 1, bass.ds(tile, 1), :]
                    cn3 = c_n[b].rearrange("p (a d) -> p a d", a=1)
                    nc.vector.tensor_copy(v_hi, cn3).then_inc(val_hi, 1)
                    dve.wait_ge(val_hi, c * 4 + t + 1)
                    nc.vector.tensor_tensor(v_lo, cn3, stored(v_hi), ALU.subtract)
                for n, (src, dst, scale) in enumerate(chunk_splits(c)):
                    dve.wait_ge(hi_done, c * (KR + 2) + n + 1)
                    if scale is None:
                        nc.vector.tensor_tensor(dst(1), src, stored(dst(0)), ALU.subtract).then_inc(lo_done, 1)
                    else:
                        nc.vector.scalar_tensor_tensor(out=dst(1), in0=src, scalar=scale, in1=stored(dst(0)),
                                                       op0=ALU.mult, op1=ALU.subtract).then_inc(lo_done, 1)
                dve.wait_ge(cq_stored, c * 16 + 16)


def attention_phase(nc, m):
    with ExitStack() as ctx:
        def sb(name, shape, dt=F32):
            return ctx.enter_context(nc.sbuf_tensor(name, shape, dt))

        def sem(name):
            return ctx.enter_context(nc.semaphore(name))

        even = m.pool[:, 0:HG * (NT - 1) * P].rearrange("p (h k) -> p h k", h=HG)
        odd = m.pool[:, HG * (NT - 1) * P:].rearrange("p (h k) -> p h k", h=HG)
        probs = [even, odd]
        q_c = sb("q_c", [P, 2, HG, 512], F32R)
        q_pe = sb("q_pe", [P, HG, 512], F32R)
        turned_p = sb("turned_p", [P, 2, 2, 512], F32R)
        o_t = sb("o_t", [P, 2, 512], F32R)
        y = sb("y", [P, 2, HID])
        rot_cos = sb("rot_cos", [P, HG * DR])
        rot_sin = sb("rot_sin", [P, HG * DR])
        rot = sb("rot", [P, HG * P])
        half_max = m.small[:, 20:22]
        neg_max = m.small[:, 24:24 + HG]
        half_sum = m.small[:, 28:28 + 2 * HG]
        row_sum = m.small[:, 36:36 + HG]
        inv_sum = m.small[:, 40:40 + HG]
        TURN, OUT, MISC = [m.bank[4], m.bank[5]], m.bank[6], m.bank[7]

        wq_loaded = sem("wq_loaded")
        wo_loaded = sem("wo_loaded")
        cq_loaded = sem("cq_loaded")
        y_loaded = [sem(f"y_loaded{n}") for n in range(2)]
        y_stored = m.y_stored
        y_added = sem("y_added")
        scores_ready = sem("scores_ready")
        half_max_done = sem("half_max_done")
        max_done = sem("max_done")
        exp_done = sem("exp_done")
        sum_done = sem("sum_done")
        inv_done = sem("inv_done")
        norm_done = sem("norm_done")
        p_turned = sem("p_turned")
        p_hi = sem("p_hi")
        p_lo = sem("p_lo")
        pv_done = sem("pv_done")
        o_hi = sem("o_hi")
        o_lo = sem("o_lo")
        misc_ready = sem("misc_ready")
        q_hi = sem("q_hi")
        q_lo = sem("q_lo")
        rope_cos = sem("rope_cos")
        rope_sum = sem("rope_sum")
        rope_hi = sem("rope_hi")
        rope_lo = sem("rope_lo")
        qpe_done = sem("qpe_done")

        def banks(i):
            return (i + 4) // 4

        def width(i):
            return (i + 1) * P

        def place(i, h):
            return h % (4 // banks(i)) * banks(i)

        def parts(i):
            w = width(i)
            return [(0, w)] if banks(i) <= 2 else [(0, 1024), (1024, w)]

        def score_count(i, h, b):
            return 4 * sum(banks(n) for n in range(i)) + h * banks(i) + b + 1

        def part_count(i, h, a):
            return 4 * sum(len(parts(n)) for n in range(i)) + h * len(parts(i)) + a + 1

        def two_part_count(i, h):
            return 4 * sum(len(parts(n)) == 2 for n in range(i)) + (h + 1)

        def head_count(i, h):
            return 4 * i + h + 1

        def key_count(i, j):
            return i * (i + 1) // 2 + j + 1

        SCORES, PARTS, HEADS, KEYS = score_count(NT, 0, -1), part_count(NT, 0, -1), 4 * NT, key_count(NT, -1)
        TWO = two_part_count(NT, -1)

        def quarter(i, h):
            n = i + 1
            return range(h * n // 4, (h + 1) * n // 4)

        uses = []
        for h in range(HG):
            uses.append(("q", 0, h))
        for t in range(3):
            uses += [("pe", t), ("turn", t)]
        for i in range(NT):
            for h in range(HG):
                if h == 0 and i >= 2:
                    uses.append(("y", i - 2))
                if i % 4 == 3 and i < NT - 1:
                    uses.append(("q", i // 4 + 1, h))
                if i + 3 < NT and h == 1:
                    uses.append(("pe", i + 3))
                if i + 3 < NT and h == 3:
                    uses.append(("turn", i + 3))
        uses += [("y", NT - 2), ("y", NT - 1)]
        use = {u: n for n, u in enumerate(uses)}
        USES = len(uses)

        block = ctx.enter_context(nc.Block())

        @block.sync
        def _(sp):
            def load_cq(c):
                sp.dma_start(words(m.cq), m.cq_dram[c]
                             ).then_inc(cq_loaded, 16)

            def load_y(i):
                sp.dma_start(y[:, i % 2, :], m.y_dram[i]).then_inc(y_loaded[i % 2], 16)

            def store_y(g, i):
                sp.wait_ge(y_added, g * NT + i + 1)
                sp.dma_start(m.y_dram[i], y[:, i % 2, :]).then_inc(y_stored, 16)

            load_cq(0)
            with sp.Fori(0, G) as g:
                sp.dma_start(words(m.wo), m.wo_dram[g]
                             ).then_inc(wo_loaded, 16)
                for i in range(NT):
                    if i == 1:
                        sp.wait_ge(y_stored, g * (16 * NT) + 16)
                    if i >= 3:
                        sp.wait_ge(y_stored, g * (16 * NT) + 16 * (i - 1))
                    if i >= 1:
                        load_y(i - 1)
                    if i >= 2:
                        store_y(g, i - 2)
                    if i % 4 == 0:
                        sp.wait_ge(misc_ready, g * USES + use["pe", i + 3] + 1)
                        load_cq((i // 4 + 1) % NCH)
                sp.wait_ge(y_stored, g * (16 * NT) + 16 * (NT - 1))
                load_y(NT - 1)
                store_y(g, NT - 2)
                store_y(g, NT - 1)
            sp.wait_ge(y_stored, 16 * (NT * G + 1))
            sp.wait_ge(wq_loaded, 16 * G)
            sp.wait_ge(cq_loaded, 16 * (NCH * G + 1))

        @block.tensor
        def _(pe):
            with pe.Fori(0, G) as g:
                def wait_read(u):
                    if u[0] == "q":
                        pe.wait_ge(q_lo, g * (NCH * HG) + u[1] * HG + u[2] + 1)
                    elif u[0] == "pe":
                        pe.wait_ge(rope_cos, g * (3 * NT) + 3 * u[1] + 3)
                    elif u[0] == "turn":
                        pe.wait_ge(qpe_done, g * NT + u[1] + 1)
                    else:
                        pe.wait_ge(y_added, g * NT + u[1] + 1)

                def shared(u):
                    if use[u]:
                        wait_read(uses[use[u] - 1])

                def project_q(c, h):
                    shared(("q", c, h))
                    n = 0
                    for k in range(KR):
                        for a, b in ((0, 0), (1, 0), (0, 1)):
                            mm = pe.matmul(MISC, m.wq[:, a, k, h * C:h * C + C], m.cq[:, b, k, :],
                                           start=(n == 0), stop=(n == 3 * KR - 1))
                            n += 1
                    mm.then_inc(misc_ready, 1)

                def project_pe(t):
                    shared(("pe", t))
                    n = 0
                    for k in range(KR):
                        for a, b in ((0, 0), (1, 0), (0, 1)):
                            mm = pe.matmul(MISC[:, 0:HG * DR], m.cq[:, a, k, t % 4 * P:t % 4 * P + P],
                                           m.wq[:, b, k, HG * C:WCOL], start=(n == 0), stop=(n == 3 * KR - 1))
                            n += 1
                    mm.then_inc(misc_ready, 1)

                def turn_pe(t):
                    shared(("turn", t))
                    pe.wait_ge(rope_lo, g * NT + t + 1)
                    for h in range(HG):
                        mm = pe.transpose(MISC[:, h * P:h * P + P], rot[:, h * P:h * P + P], m.ident[:, :])
                    mm.then_inc(misc_ready, 1)

                def scores(i, h):
                    t = i % 4 * P
                    if h == 0:
                        if i % 4 == 0:
                            pe.wait_ge(q_lo, g * (NCH * HG) + (i // 4) * HG + HG)
                        pe.wait_ge(qpe_done, g * NT + i + 1)
                    mine = set(range(place(i, h), place(i, h) + banks(i)))
                    n = 4 * i + h - 1
                    while n >= 0 and not mine & set(range(place(n // 4, n % 4),
                                                          place(n // 4, n % 4) + banks(n // 4))):
                        n -= 1
                    for b in range(banks(i)):
                        if n >= 0:
                            pi, ph = n // 4, n % 4
                            last = len(parts(pi)) - 1
                            if banks(i) == 4 and banks(pi) >= 3:
                                a = b // 2
                                if b % 2 == 0:
                                    pe.wait_ge(exp_done, g * PARTS + part_count(pi, ph, min(a, last)))
                            elif b == 0:
                                pe.wait_ge(exp_done, g * PARTS + part_count(pi, ph, last))
                        k0 = b * 512
                        n_k = min(512, width(i) - k0)
                        diagonal = b == banks(i) - 1
                        out = m.bank[place(i, h) + b]
                        row = out[:, 0:n_k]
                        terms = [(q_c[:, 0, h, t:t + P], m.key_c[:, 0, k0:k0 + n_k]),
                                 (q_c[:, 0, h, t:t + P], m.key_c[:, 1, k0:k0 + n_k]),
                                 (q_c[:, 1, h, t:t + P], m.key_c[:, 0, k0:k0 + n_k]),
                                 (q_pe[:, h, t:t + P], m.key_pe[:, 0, k0:k0 + n_k]),
                                 (q_pe[:, h, t:t + P], m.key_pe[:, 1, k0:k0 + n_k])]
                        for x, (q, k) in enumerate(terms):
                            mm = pe.matmul(row, q, k, start=(x == 0), stop=(x == 4 and not diagonal))
                        if diagonal:
                            mm = pe.matmul(row[:, n_k - P:n_k], m.ident16[:, :], m.mask16[:, :],
                                           start=False, stop=True)
                        mm.then_inc(scores_ready, 1)

                def turn_probs(i, j):
                    if j == 0:
                        pe.wait_ge(norm_done, g * HEADS + head_count(i, HG - 1))
                    n = key_count(i, j)
                    if n > 2:
                        pe.wait_ge(p_lo, g * KEYS + n - 2)
                    for h in range(HG):
                        mm = pe.transpose(TURN[n % 2][:, h * P:h * P + P], probs[i % 2][:, h, j * P:j * P + P],
                                          m.ident[:, :])
                    mm.then_inc(p_turned, 1)

                def values(i, j):
                    if j == 0 and i > 0:
                        pe.wait_ge(o_lo, g * NT + i)
                    n = key_count(i, j)
                    pe.wait_ge(p_hi, g * KEYS + n)
                    pe.matmul(OUT, m.val[:, 0, j, :], turned_p[:, n % 2, 0, :], start=(j == 0), stop=False)
                    pe.matmul(OUT, m.val[:, 1, j, :], turned_p[:, n % 2, 0, :], start=False, stop=False)
                    pe.wait_ge(p_lo, g * KEYS + n)
                    pe.matmul(OUT, m.val[:, 0, j, :], turned_p[:, n % 2, 1, :], start=False,
                              stop=(j == i)).then_inc(pv_done, 1)

                def project_out(i):
                    shared(("y", i))
                    if i == 0:
                        pe.wait_ge(wo_loaded, g * 16 + 16)
                    pe.wait_ge(o_lo, g * NT + i + 1)
                    n = 0
                    for h in range(HG):
                        for a, b in ((0, 0), (0, 1), (1, 0)):
                            mm = pe.matmul(MISC, o_t[:, a, h * P:h * P + P], m.wo[:, b, h, :],
                                           start=(n == 0), stop=(n == 3 * HG - 1))
                            n += 1
                    mm.then_inc(misc_ready, 1)

                pe.wait_ge(wq_loaded, g * 16 + 16)
                pe.wait_ge(cq_loaded, g * (16 * NCH) + 16)
                for h in range(HG):
                    project_q(0, h)
                for t in range(3):
                    project_pe(t)
                    turn_pe(t)
                for i in range(NT):
                    if i >= 1:
                        turn_probs(i - 1, 0)
                    for h in range(HG):
                        scores(i, h)
                        if h == 0 and i >= 2:
                            project_out(i - 2)
                        if i >= 1:
                            for j in quarter(i - 1, h):
                                if j < i - 1:
                                    turn_probs(i - 1, j + 1)
                                values(i - 1, j)
                        if i % 4 == 3 and i < NT - 1:
                            if h == 0:
                                pe.wait_ge(cq_loaded, g * (16 * NCH) + 16 * (i // 4 + 2))
                            project_q(i // 4 + 1, h)
                        if i + 3 < NT and h == 1:
                            if i % 4 == 1:
                                pe.wait_ge(cq_loaded, g * (16 * NCH) + 16 * (i // 4 + 2))
                            project_pe(i + 3)
                        if i + 3 < NT and h == 3:
                            turn_pe(i + 3)
                i = NT - 1
                turn_probs(i, 0)
                project_out(i - 1)
                for j in range(NT):
                    if j < i:
                        turn_probs(i, j + 1)
                    values(i, j)
                project_out(i)
                wait_read(uses[-1])

        def steps(first_turn, head, after_turn, other):
            for h in range(HG):
                other(("q", 0, h))
            for t in range(3):
                other(("pe", t))
                other(("turn", t))
            for i in range(NT):
                if i >= 1:
                    first_turn(i - 1)
                for h in range(HG):
                    keys = [j for j in quarter(i - 1, h) if j < i - 1] if i else []
                    if h == 0 and i >= 2:
                        head(i, h, keys, lambda: other(("y", i - 2)))
                    else:
                        head(i, h, keys, None)
                    if i % 4 == 3 and i < NT - 1:
                        other(("q", i // 4 + 1, h))
                    if i + 3 < NT and h == 1:
                        other(("pe", i + 3))
                    if i + 3 < NT and h == 3:
                        other(("turn", i + 3))
                if i >= 1:
                    after_turn(i - 1)
            i = NT - 1
            first_turn(i)
            other(("y", i - 1))
            head(None, None, list(range(i)), None)
            after_turn(i)
            other(("y", i))

        @block.scalar
        def _(act):
            with act.Fori(0, G) as g:
                def hi(i, j):
                    n = key_count(i, j)
                    act.wait_ge(p_turned, g * KEYS + n)
                    nc.scalar.copy(turned_p[:, n % 2, 0, :], TURN[n % 2]).then_inc(p_hi, 1)

                def exps(i, h, a):
                    lo, up = parts(i)[a]
                    if a == 0:
                        act.wait_ge(max_done, g * HEADS + head_count(i, h))
                    row = m.rows[:, place(i, h) * 512 + lo:place(i, h) * 512 + up]
                    nc.scalar.activation(probs[i % 2][:, h, lo:up], row, ACT.Exp, bias=neg_max[:, h:h + 1],
                                         accum_out=half_sum[:, 2 * h + a:2 * h + a + 1]).then_inc(exp_done, 1)

                def head(i, h, keys, _):
                    todo = [(i, h, a) for a in range(len(parts(i)))] if i is not None else []
                    row = NT - 1 if i is None else i - 1
                    for n, j in enumerate(keys):
                        hi(row, j + 1)
                        if todo:
                            exps(*todo.pop(0))
                    for x in todo:
                        exps(*x)

                def after_turn(i):
                    act.wait_ge(pv_done, g * KEYS + key_count(i, i))
                    nc.scalar.copy(o_t[:, 0, :], OUT).then_inc(o_hi, 1)

                def other(u):
                    if u[0] == "q":
                        act.wait_ge(misc_ready, g * USES + use[u] + 1)
                        nc.scalar.copy(q_c[:, 0, u[2], :], MISC).then_inc(q_hi, 1)
                    elif u[0] == "pe":
                        act.wait_ge(rope_sum, g * (2 * NT) + 2 * u[1] + 2)
                        nc.scalar.copy(rot[:, :].bitcast(F32R).rearrange("p (h a d) -> p h a d", h=HG, a=2)[:, :, 0, :],
                                       rot_cos[:, :].rearrange("p (h d) -> p h d", h=HG)).then_inc(rope_hi, 1)
                    elif u[0] == "turn":
                        t = u[1] % 4 * P
                        act.wait_ge(misc_ready, g * USES + use[u] + 1)
                        nc.scalar.copy(q_pe[:, :, t:t + P], MISC.rearrange("p (h n) -> p h n", h=HG))\
                            .then_inc(qpe_done, 1)

                steps(lambda i: hi(i, 0), head, after_turn, other)

        @block.gpsimd
        def _(pool):
            hi = rot[:, :].rearrange("p (h a d) -> p h a d", h=HG, a=2)[:, :, 0, :]
            lo = rot[:, :].rearrange("p (h a d) -> p h a d", h=HG, a=2)[:, :, 1, :]
            ca = rot_cos[:, :].rearrange("p (h a d) -> p h a d", h=HG, a=2)
            sa = rot_sin[:, :].rearrange("p (h a d) -> p h a d", h=HG, a=2)
            def rotate(t):
                pool.wait_ge(rope_cos, t * 3 + 3)
                nc.gpsimd.tensor_tensor(ca[:, :, 0, :], ca[:, :, 0, :], sa[:, :, 0, :], ALU.subtract
                                        ).then_inc(rope_sum, 1)
                nc.gpsimd.tensor_tensor(ca[:, :, 1, :], ca[:, :, 1, :], sa[:, :, 1, :], ALU.add
                                        ).then_inc(rope_sum, 1)
                pool.wait_ge(rope_hi, t + 1)
                nc.gpsimd.tensor_tensor(lo, rot_cos[:, :].rearrange("p (h d) -> p h d", h=HG), hi,
                                        ALU.subtract).then_inc(rope_lo, 1)

            pool.dma_start(words(m.wq), m.wq_dram[0]).then_inc(wq_loaded, 16)
            with pool.Fori(0, G - 1) as g:
                with pool.Fori(0, NT) as t:
                    rotate(g * NT + t)
                pool.wait_ge(misc_ready, g * USES + use["pe", NT - 1] + 1)
                pool.dma_start(words(m.wq), m.wq_dram[g + 1]).then_inc(wq_loaded, 16)
            with pool.Fori((G - 1) * NT, G * NT) as t:
                rotate(t)

        @block.vector
        def _(dve):
            with dve.Fori(0, G) as g:
                def lo(i, j):
                    n = key_count(i, j)
                    dve.wait_ge(p_hi, g * KEYS + n)
                    nc.vector.tensor_tensor(turned_p[:, n % 2, 1, :], TURN[n % 2], stored(turned_p[:, n % 2, 0, :]),
                                            ALU.subtract).then_inc(p_lo, 1)

                def maxima(i, h):
                    first = place(i, h) * 512
                    for a, (c0, c1) in enumerate(parts(i)):
                        dve.wait_ge(scores_ready, g * SCORES + score_count(i, h, (c1 - 1) // 512))
                        row = m.rows[:, first + c0:first + c1]
                        if len(parts(i)) == 1:
                            nc.vector.tensor_reduce(neg_max[:, h:h + 1], row, AX.X, ALU.max, negate=True
                                                    ).then_inc(max_done, 1)
                        else:
                            nc.vector.tensor_reduce(half_max[:, a:a + 1], row, AX.X, ALU.max
                                                    ).then_inc(half_max_done, 1)
                    if len(parts(i)) == 2:
                        dve.wait_ge(half_max_done, g * (2 * TWO) + 2 * two_part_count(i, h))
                        nc.vector.tensor_reduce(neg_max[:, h:h + 1], half_max, AX.X, ALU.max, negate=True
                                                ).then_inc(max_done, 1)

                def normalise(i, h):
                    last = len(parts(i)) - 1
                    dve.wait_ge(exp_done, g * PARTS + part_count(i, h, last))
                    total = half_sum[:, 2 * h:2 * h + 1]
                    if last:
                        total = row_sum[:, h:h + 1]
                        nc.vector.tensor_reduce(total, half_sum[:, 2 * h:2 * h + 2], AX.X, ALU.add
                                                ).then_inc(sum_done, 1)
                        dve.wait_ge(sum_done, g * TWO + two_part_count(i, h))
                    nc.vector.reciprocal(inv_sum[:, h:h + 1], total).then_inc(inv_done, 1)
                    dve.wait_ge(inv_done, g * HEADS + head_count(i, h))
                    p = probs[i % 2][:, h, 0:width(i)]
                    nc.vector.tensor_scalar(p, p, inv_sum[:, h:h + 1], None, ALU.mult).then_inc(norm_done, 1)

                def head(i, h, keys, late):
                    if i is not None:
                        maxima(i, h)
                    if late:
                        late()
                    row = NT - 1 if i is None else i - 1
                    for j in keys:
                        lo(row, j + 1)
                    if i is not None:
                        normalise(i, h)

                def after_turn(i):
                    dve.wait_ge(o_hi, g * NT + i + 1)
                    nc.vector.tensor_tensor(o_t[:, 1, :], OUT, stored(o_t[:, 0, :]), ALU.subtract).then_inc(o_lo, 1)

                def other(u):
                    if u[0] == "q":
                        _, c, h = u
                        dve.wait_ge(q_hi, g * (NCH * HG) + c * HG + h + 1)
                        nc.vector.tensor_tensor(q_c[:, 1, h, :], MISC, stored(q_c[:, 0, h, :]), ALU.subtract)\
                            .then_inc(q_lo, 1)
                    elif u[0] == "pe":
                        t = u[1]
                        dve.wait_ge(misc_ready, g * USES + use[u] + 1)
                        q = MISC[:, 0:HG * DR].rearrange("p (h a d) -> p h a d", h=HG, a=2)
                        ca = rot_cos[:, :].rearrange("p (h d) -> p h d", d=HALF)
                        sa = rot_sin[:, :].rearrange("p (h a d) -> p h a d", h=HG, a=2)
                        cos_t = m.cos[:, t:t + 1, :].broadcast_to([P, 2 * HG, HALF])
                        sin_t = m.sin[:, t:t + 1, :].broadcast_to([P, HG, HALF])
                        nc.vector.tensor_tensor(ca, MISC[:, 0:HG * DR].rearrange("p (h d) -> p h d", d=HALF), cos_t,
                                                ALU.mult).then_inc(rope_cos, 1)
                        nc.vector.tensor_tensor(sa[:, :, 0, :], q[:, :, 1, :], sin_t, ALU.mult).then_inc(rope_cos, 1)
                        nc.vector.tensor_tensor(sa[:, :, 1, :], q[:, :, 0, :], sin_t, ALU.mult)\
                            .then_inc(rope_cos, 1)
                    elif u[0] == "y":
                        i = u[1]
                        dve.wait_ge(misc_ready, g * USES + use[u] + 1)
                        dve.wait_ge(y_loaded[i % 2], g * (8 * NT) + 16 * (i // 2 + 1))
                        nc.vector.tensor_tensor(y[:, i % 2, :], MISC, y[:, i % 2, :], ALU.add)\
                            .then_inc(y_added, 1)

                steps(lambda i: lo(i, 0), head, after_turn, other)


def ffn_phase(nc, m, w, scale_w, bias, out):
    with ExitStack() as ctx:
        def sem(name):
            return ctx.enter_context(nc.semaphore(name))

        at = 0

        def stage(n):
            nonlocal at
            at += n
            return m.pool[:, at - n:at]

        w_rows = stage(KH * HID).rearrange("p (o i) -> p o i", o=KH)
        w_s = stage(KH * HID).rearrange("p (o i) -> p o i", o=KH)
        w_t = stage(KH * HID).rearrange("p (k o) -> p k o", k=KH)
        bias_rows = stage(HID)
        y_in = [stage(HID) for _ in range(2)]
        x1 = [stage(HID) for _ in range(2)]
        x1b = [stage(HID) for _ in range(2)]
        x1_t = [stage(HID) for _ in range(2)]
        z = [stage(HID) for _ in range(2)]
        o_out = [stage(HID) for _ in range(2)]
        w_scale = m.small[:, 0:4]
        eps = m.small[:, 4:5]
        spare = m.small[:, 5:6]
        stats = [stage(8) for _ in range(4)]
        agg = [stage(2) for _ in range(4)]
        dev = [stage(1) for _ in range(4)]
        inv = [stage(1) for _ in range(4)]

        w_loaded = sem("ffn_w_loaded")
        w_scaled = sem("ffn_w_scaled")
        w_turned = sem("ffn_w_turned")
        w_copied = sem("ffn_w_copied")
        eps_set = sem("eps_set")
        yin_loaded = [sem(f"yin_loaded{n}") for n in range(2)]
        normed = sem("normed")
        stat_step = sem("stat_step")
        dev_done = sem("dev_done")
        x1_done = sem("x1_done")
        x1b_done = sem("x1b_done")
        x1_turned = sem("x1_turned")
        x1t_copied = sem("x1t_copied")
        lin_ready = sem("lin_ready")
        z_done = sem("z_done")
        out_done = sem("out_done")
        out_stored = [sem(f"out_stored{n}") for n in range(2)]

        block = ctx.enter_context(nc.Block())
        out_v = out.rearrange("(t p) d -> t p d", p=P)
        TURNS = NT // 2

        @block.sync
        def _(sp):
            sp.dma_start(w_rows, w.rearrange("(o p) i -> p o i", p=P)).then_inc(w_loaded, 16)
            sp.dma_start(w_scale, scale_w.rearrange("(o p) -> p o", p=P),
                         allow_slow_non_contiguous=True).then_inc(w_loaded, 16)
            sp.dma_start(bias_rows, bias.rearrange("(a d) -> a d", a=1).broadcast_to([P, HID])).then_inc(w_loaded, 16)

        @block.gpsimd
        def _(pool):
            for b in range(2):
                pool.dma_start(y_in[b], m.y_dram[b]).then_inc(yin_loaded[b], 16)
            pool.wait_ge(w_loaded, 48)
            def add_bias(n, b):
                pool.wait_ge(x1_done, n * 2 + b + 1)
                nc.gpsimd.tensor_tensor(x1b[b], x1[b], bias_rows, ALU.add).then_inc(x1b_done, 1)

            def store(n, b):
                pool.wait_ge(out_done, n * 2 + b + 1)
                pool.dma_start(out_v[2 * n + b], o_out[b]).then_inc(out_stored[b], 16)

            with pool.Fori(0, TURNS - 1) as n:
                for b in range(2):
                    add_bias(n, b)
                    pool.dma_start(y_in[b], m.y_dram[2 * n + 2 + b]).then_inc(yin_loaded[b], 16)
                for b in range(2):
                    store(n, b)
            for b in range(2):
                add_bias(TURNS - 1, b)
            for b in range(2):
                store(TURNS - 1, b)
            for b in range(2):
                pool.wait_ge(out_stored[b], 16 * TURNS)

        @block.tensor
        def _(pe):
            pe.wait_ge(w_scaled, KH)
            for k in range(KH):
                for o in range(KH):
                    mm = pe.transpose(m.bank[k][:, o * P:o * P + P], w_s[:, o, k * P:k * P + P], m.ident[:, :])
            mm.then_inc(w_turned, 1)
            pe.wait_ge(w_copied, KH)
            with pe.Fori(0, TURNS) as n:
                for b in range(2):
                    pe.wait_ge(x1_done, n * 2 + b + 1)
                    for k in range(KH):
                        mm = pe.transpose(m.bank[b][:, k * P:k * P + P], x1[b][:, k * P:k * P + P], m.ident[:, :])
                    mm.then_inc(x1_turned, 1)
                for b in range(2):
                    pe.wait_ge(x1t_copied, n * 2 + b + 1)
                    for k in range(KH):
                        mm = pe.matmul(m.bank[2 + b], x1_t[b][:, k * P:k * P + P], w_t[:, k, :],
                                       start=(k == 0), stop=(k == KH - 1))
                    mm.then_inc(lin_ready, 1)
                pe.wait_ge(z_done, n * 2 + 2)

        @block.scalar
        def _(act):
            act.wait_ge(w_loaded, 48)
            for o in range(KH):
                nc.scalar.activation(w_s[:, o, :], w_rows[:, o, :], ACT.Copy, scale=w_scale[:, o:o + 1]
                                     ).then_inc(w_scaled, 1)
            act.wait_ge(w_turned, 1)
            for k in range(KH):
                nc.scalar.copy(w_t[:, k, :], m.bank[k]).then_inc(w_copied, 1)
            act.wait_ge(eps_set, 1)
            with act.Fori(0, TURNS) as n:
                def root(slot, count):
                    act.wait_ge(stat_step, count)
                    nc.scalar.activation(dev[slot], agg[slot][:, 1:2], ACT.Sqrt, bias=eps).then_inc(dev_done, 1)

                for b in range(2):
                    root(b, n * 12 + 3 * b + 2)
                for b in range(2):
                    act.wait_ge(x1_turned, n * 2 + b + 1)
                    nc.scalar.copy(x1_t[b], m.bank[b]).then_inc(x1t_copied, 1)
                for b in range(2):
                    root(2 + b, n * 12 + 6 + 3 * b + 2)

        @block.vector
        def _(dve):
            nc.vector.memset(eps, LN_EPS).then_inc(eps_set, 1)
            with dve.Fori(0, TURNS) as n:
                def norm(src, dst, slot, done, count):
                    nc.vector.bn_stats(stats[slot][:, 0:6], src).then_inc(stat_step, 1)
                    dve.wait_ge(stat_step, count + 1)
                    nc.vector.memset(spare, 0.0)
                    nc.vector.bn_aggr(agg[slot], stats[slot][:, 0:6]).then_inc(stat_step, 1)
                    dve.wait_ge(dev_done, n * 4 + slot + 1)
                    nc.vector.reciprocal(inv[slot], dev[slot]).then_inc(stat_step, 1)
                    dve.wait_ge(stat_step, count + 3)
                    nc.vector.tensor_scalar(dst, src, agg[slot][:, 0:1], inv[slot], ALU.subtract, ALU.mult
                                            ).then_inc(done, 1)

                for b in range(2):
                    dve.wait_ge(yin_loaded[b], n * 16 + 16)
                    norm(y_in[b], x1[b], b, x1_done, n * 12 + 3 * b)
                for b in range(2):
                    dve.wait_ge(lin_ready, n * 2 + b + 1)
                    dve.wait_ge(x1b_done, n * 2 + b + 1)
                    nc.vector.tensor_tensor(z[b], m.bank[2 + b], x1b[b], ALU.add).then_inc(z_done, 1)
                    dve.wait_ge(z_done, n * 2 + b + 1)
                    norm(z[b], o_out[b], 2 + b, out_done, n * 12 + 6 + 3 * b)
                for b in range(2):
                    dve.wait_ge(out_stored[b], n * 16 + 16)


def build(nc, x, w_qa, q_ln, w_qb, w_kva, kv_ln, w_kvb, w_o, ffn_w, ffn_scale, ffn_bias,
          ident_in, mask_in, cos_in, sin_in, out):
    with ExitStack() as ctx:
        m = Memory(nc, ctx)
        x2, out2 = x[0], out[0]
        weights_phase(nc, m, x2, w_qb, w_kvb, w_o, q_ln, kv_ln, ident_in, mask_in, cos_in, sin_in)
        tokens_phase(nc, m, x2, w_qa, w_kva)
        attention_phase(nc, m)
        ffn_phase(nc, m, ffn_w, ffn_scale, ffn_bias, out2)


_INS = ['L0_attn_hidden_states', 'L0_attn_w_qa', 'L0_attn_q_a_ln_w', 'L0_attn_w_qb', 'L0_attn_w_kva',
        'L0_attn_kv_a_ln_w', 'L0_attn_w_kvb', 'L0_attn_w_o', 'L0_ffn_weight', 'L0_ffn_scale_weight',
        'L0_ffn_bias']


def _constants():
    inv_freq = (1.0 / np.float32(10000.0) ** (np.arange(0, DR, 2, dtype=np.float32) / np.float32(DR))).astype(np.float32)
    angle = np.outer(np.arange(S, dtype=np.float32), inv_freq).astype(np.float32)
    return {
        "ident": np.eye(P, dtype=np.float32),
        "mask": np.triu(np.full((P, P), MASKED, np.float32), k=1),
        "cos": np.cos(angle).astype(np.float32),
        "sin": np.sin(angle).astype(np.float32),
    }


def kernel(**inputs):
    import numpy as _np
    import concourse.bacc as _bacc
    from concourse import mybir as _mybir
    from concourse.bass_utils import run_bass_kernel_spmd as _run

    nc = _bacc.Bacc("TRN2", target_bir_lowering=False, num_devices=1)
    arrays, args = {}, []
    named = {f"in_{n}": _np.ascontiguousarray(inputs[n]) for n in _INS}
    named.update({f"const_{n}": a for n, a in _constants().items()})
    for name, a in named.items():
        arrays[name] = a
        args.append(nc.dram_tensor(name, a.shape, _mybir.dt.from_np(a.dtype), kind="ExternalInput").ap())
    out = nc.dram_tensor("out_dram", (1, S, HID), _mybir.dt.float32, kind="ExternalOutput").ap()
    build(nc, *args, out)
    r = _run(nc, [arrays], core_ids=[0])
    return r.results[0]["out_dram"]
```

```python
from contextlib import ExitStack

import numpy as np

import concourse.bass as bass
from concourse import mybir

F32 = mybir.dt.float32
F32R = mybir.dt.float32r
BF16 = mybir.dt.bfloat16
ALU = mybir.AluOpType
ACT = mybir.ActivationFunctionType
AX = mybir.AxisListType

P = 128
S = 2048
HID = 512
H = 16
QLR = 384
C = 128
DN, DR, DV = 128, 64, 128
DQ = DN + DR
HALF = DR // 2
SCALE = DQ ** -0.5
RMS_EPS, LN_EPS = 1e-6, 1e-5
MASKED = -1e38

NT = S // P
NCH = NT // 4
G = 4
HG = H // G
KR = QLR // P
KH = HID // P
WCOL = HG * C + HG * DR
PAIRS = HG // 2


def stored(view):
    return view.bitcast(F32)


def words(buffer):
    return stored(buffer[:, :, :, :].rearrange("p a k n -> p (a k n)"))


class Memory:

    def __init__(self, nc, ctx):
        def sb(name, shape, dt=F32):
            return ctx.enter_context(nc.sbuf_tensor(name, shape, dt))

        self.bank = [ctx.enter_context(nc.psum_tensor(f"bank{n}", [P, 512], F32)) for n in range(4, 8)]
        self.rows = ctx.enter_context(nc.psum_tensor("rows", [P, 4 * 512], F32))
        self.bank = [self.rows[:, 512 * n:512 * n + 512] for n in range(4)] + [b[:, :] for b in self.bank]

        self.key_c = sb("key_c", [P, 2, S], F32R)
        self.key_pe = sb("key_pe", [P, 2, S], F32R)
        self.val = sb("val", [P, 2, NT, C], F32R)
        self.cq = sb("cq", [P, 2, KR, 512], F32R)
        self.wq = sb("wq", [P, 2, KR, WCOL], F32R)
        self.wo = sb("wo", [P, 2, HG, HID], F32R)
        self.ident = sb("ident", [P, P])
        self.ident16 = sb("ident16", [P, P], BF16)
        self.mask16 = sb("mask16", [P, P], BF16)
        self.cos = sb("cos", [P, NT, HALF])
        self.sin = sb("sin", [P, NT, HALF])
        self.small = sb("small", [P, 64])
        self.pool = sb("pool", [P, HG * (NT - 1) * P + HG * NT * P])

        self.cq_dram = nc.dram_tensor("cq_dram", (NCH, P, 2 * KR * 512), F32, kind="Internal").ap()
        self.wq_dram = nc.dram_tensor("wq_dram", (G, P, 2 * KR * WCOL), F32, kind="Internal").ap()
        self.wo_dram = nc.dram_tensor("wo_dram", (G, P, 2 * HG * HID), F32, kind="Internal").ap()
        self.y_stored = ctx.enter_context(nc.semaphore("y_stored"))
        self.y_dram = nc.dram_tensor("y_dram", (NT, P, HID), F32, kind="Internal").ap()


def prepare_phase(nc, m, x, w_qa, w_kva, w_qb, w_kvb, w_o, q_ln, kv_ln, ident_in, mask_in, cos_in, sin_in):
    with ExitStack() as ctx:
        def sem(name):
            return ctx.enter_context(nc.semaphore(name))

        at = 0

        def stage(n):
            nonlocal at
            at += n
            return m.pool[:, at - n:at]

        def sb(name, n):
            return ctx.enter_context(nc.sbuf_tensor(name, [P, n], F32))[:, :]

        WA = QLR + C + DR
        nope = stage(HG * QLR).rearrange("p (h r) -> p h r", h=HG)
        pe_rows = stage(PAIRS * QLR).rearrange("p (a r) -> p a r", a=PAIRS)
        kv = stage(HG * 2 * C).rearrange("p (h k c) -> p h k c", h=HG, k=2)
        wo_rows = stage(KH * HG * DV).rearrange("p (o d) -> p o d", o=KH)
        wo_t = stage(HG * HID).rearrange("p (h o) -> p h o", h=HG)
        mask = stage(P)
        wa_t = stage(KH * WA).rearrange("p (k n) -> p k n", k=KH)
        x_in = stage(4 * HID).rearrange("p (t i) -> p t i", t=4)
        x_t = [stage(HID) for _ in range(2)]
        cq_n = [stage(QLR) for _ in range(2)]
        wa_rows = sb("wa_rows", 4 * HID).rearrange("p (o i) -> p o i", o=4)
        wa_tail = sb("wa_tail", HID)
        squares = sb("squares", QLR + C)
        c_n = [sb(f"c_n{b}", C) for b in range(2)]
        k_rot = [sb(f"k_rot{b}", P) for b in range(2)]
        t_cos = sb("t_cos", DR)
        t_sin = sb("t_sin", DR)
        q_w = m.small[:, 0:KR]
        kv_w = m.small[:, 4:5]
        minus_half = m.small[:, 6:8]
        means = m.small[:, 8:12]
        safe = m.small[:, 12:16]
        rstd = m.small[:, 16:20]

        const_loaded = sem("const_loaded")
        consts_made = sem("consts_made")
        wa_loaded = sem("wa_loaded")
        wa_turned = sem("wa_turned")
        wa_copied = sem("wa_copied")
        x_loaded = [sem(f"x_loaded{t}") for t in range(4)]
        x_turned = sem("x_turned")
        xt_copied = sem("xt_copied")
        proj_ready = sem("proj_ready")
        squared = sem("squared")
        eps_added = sem("eps_added")
        rstd_done = sem("rstd_done")
        cqn_done = sem("cqn_done")
        cn_done = sem("cn_done")
        val_hi = sem("val_hi")
        rope_parts = sem("rope_parts")
        krot_done = sem("krot_done")
        turned = sem("turned")
        tok_hi = sem("tok_hi")
        tok_lo = sem("tok_lo")
        nope_loaded = sem("nope_loaded")
        pe_loaded = sem("pe_loaded")
        kv_loaded = sem("kv_loaded")
        wor_loaded = sem("wor_loaded")
        filled = sem("filled")
        wot_copied = sem("wot_copied")
        split_hi = sem("split_hi")
        split_lo = sem("split_lo")
        wq_free = sem("wq_free")
        wo_free = sem("wo_free")
        cq_free = sem("cq_free")

        X, PROJ, KP, TR, KT = m.bank[0:5]

        fills = [("nope", k) for k in range(KR)] + [("pe", k) for k in range(KR)] \
            + [("turn", h) for h in range(HG)] + [("out", h) for h in range(HG)]
        beside = [range(0, 3), range(3, 8), range(8, 11), range(11, 14)]
        FILLS = len(fills)
        split_of = {n: s for s, n in enumerate(n for n, f in enumerate(fills) if f[0] != "turn")}
        SPLITS = len(split_of)
        WQ_SPLITS = 2 * KR

        def fill_bank(n):
            return m.bank[5 + n % 3]

        def split_places(n):
            kind, k = fills[n]
            if kind == "nope":
                return fill_bank(n), lambda a: m.wq[:, a, k, 0:HG * C], q_w[:, k:k + 1]
            if kind == "pe":
                return fill_bank(n)[:, 0:HG * DR], lambda a: m.wq[:, a, k, HG * C:WCOL], q_w[:, k:k + 1]
            return fill_bank(n), lambda a: m.wo[:, a, k, :], kv_w

        wqb_v = w_qb.rearrange("(g h q) r -> g q h r", g=G, h=HG)
        wpe_v = w_qb.rearrange("(g a e q) r -> g e q a r", g=G, a=PAIRS, e=2)
        kvb_v = w_kvb.rearrange("(g h k d) c -> g d (h k) c", g=G, h=HG, k=2)
        wo_v = w_o.rearrange("(o p) (g n) -> g p o n", p=P, g=G)
        x_v = x.rearrange("(c t p) i -> c t p i", t=4, p=P)

        block = ctx.enter_context(nc.Block())

        @block.sync
        def _(sp):
            sp.dma_start(m.ident[:, :], ident_in).then_inc(const_loaded, 16)
            sp.dma_start(wa_rows[:, 0:3, :], w_qa.rearrange("(o p) i -> p o i", p=P)).then_inc(wa_loaded, 16)
            sp.dma_start(wa_rows[:, 3, :], w_kva[0:C]).then_inc(wa_loaded, 16)
            sp.dma_start(wa_tail[0:DR], w_kva[C:C + DR]).then_inc(wa_loaded, 16)
            sp.dma_start(q_w, q_ln.rearrange("(k p) -> p k", p=P),
                         allow_slow_non_contiguous=True).then_inc(const_loaded, 16)
            sp.dma_start(kv_w, kv_ln.rearrange("(k p) -> p k", p=P),
                         allow_slow_non_contiguous=True).then_inc(const_loaded, 16)
            sp.dma_start(mask, mask_in).then_inc(wq_free, 16)
            sp.dma_start(m.cos[:, :, :], cos_in.rearrange("(t p) d -> p t d", p=P)).then_inc(wo_free, 16)
            sp.dma_start(m.sin[:, :, :], sin_in.rearrange("(t p) d -> p t d", p=P)).then_inc(cq_free, 16)
            sp.dma_start(m.y_dram.rearrange("t p d -> (t p) d"), x).then_inc(m.y_stored, 16)

        @block.gpsimd
        def _(pool):
            def load_x(c, t):
                pool.dma_start(x_in[:, t, :], x_v[c, t]).then_inc(x_loaded[t], 16)

            def load_wq_rows(g):
                pool.dma_start(nope, wqb_v[g, 0:DN]).then_inc(nope_loaded, 16)
                for e in range(2):
                    pool.dma_start(pe_rows[DR * e:DR * e + DR], wpe_v[g, e, DN:DQ]).then_inc(pe_loaded, 16)

            def load_kv(g):
                pool.dma_start(kv.rearrange("p h k c -> p (h k) c"), kvb_v[g]).then_inc(kv_loaded, 16)

            def load_wo_rows(g):
                pool.dma_start(wo_rows, wo_v[g]).then_inc(wor_loaded, 16)

            def turn(c, more):
                for t in range(4):
                    if more:
                        pool.wait_ge(x_turned, c * 4 + t + 1)
                        load_x(c + 1, t)
                    b = t % 2
                    pool.wait_ge(eps_added, c * 4 + t + 1)
                    nc.gpsimd.tensor_tensor(rstd[:, 2 * b:2 * b + 2], safe[:, 2 * b:2 * b + 2], minus_half,
                                            ALU.pow).then_inc(rstd_done, 1)
                    if t == 2 and more:
                        pool.wait_ge(filled, c * FILLS + WQ_SPLITS)
                        load_wq_rows(c + 1)
                    if t == 3 and more:
                        pool.wait_ge(filled, c * FILLS + WQ_SPLITS + HG)
                        load_wo_rows(c + 1)
                if more:
                    pool.wait_ge(filled, c * FILLS + FILLS)
                    load_kv(c + 1)

            for t in range(4):
                load_x(0, t)
            load_wq_rows(0)
            load_kv(0)
            load_wo_rows(0)
            with pool.Fori(0, NCH - 1) as c:
                turn(c, True)
            turn(NCH - 1, False)

        @block.tensor
        def _(pe):
            pe.wait_ge(const_loaded, 16 * 3)
            pe.wait_ge(wa_loaded, 48)
            for k in range(KH):
                for o in range(4):
                    pe.transpose(m.bank[k][:, o * P:o * P + P], wa_rows[:, o, k * P:k * P + P], m.ident[:, :])
            for k in range(KH):
                mm = pe.transpose(m.bank[4][:, k * DR:k * DR + DR], wa_tail[0:DR, k * P:k * P + P],
                                  m.ident[0:DR, 0:DR])
            mm.then_inc(wa_turned, 1)
            pe.wait_ge(wa_copied, KH + 1)
            with pe.Fori(0, NCH) as c:
                def turn_x(t):
                    pe.wait_ge(x_loaded[t], c * 16 + 16)
                    if t:
                        pe.wait_ge(xt_copied, c * 4 + t)
                    for k in range(KH):
                        mm = pe.transpose(X[:, k * P:k * P + P], x_in[:, t, k * P:k * P + P], m.ident[:, :])
                    mm.then_inc(x_turned, 1)

                def project(t):
                    pe.wait_ge(xt_copied, c * 4 + t + 1)
                    if t:
                        pe.wait_ge(cn_done, c * 4 + t)
                        pe.wait_ge(rope_parts, c * 12 + 3 * t)
                    for k in range(KH):
                        pe.matmul(PROJ, x_t[t % 2][:, k * P:k * P + P], wa_t[:, k, 0:QLR + C],
                                  start=(k == 0), stop=(k == KH - 1))
                    for k in range(KH):
                        mm = pe.matmul(KP[:, 0:DR], x_t[t % 2][:, k * P:k * P + P], wa_t[:, k, QLR + C:WA],
                                       start=(k == 0), stop=(k == KH - 1))
                    mm.then_inc(proj_ready, 1)

                def turn_results(t):
                    if t:
                        pe.wait_ge(tok_lo, c * 12 + 3 * t)
                    pe.wait_ge(cqn_done, c * 4 + t + 1)
                    for k in range(KR):
                        pe.transpose(TR[:, k * P:k * P + P], cq_n[t % 2][:, k * P:k * P + P], m.ident[:, :])
                    pe.wait_ge(cn_done, c * 4 + t + 1)
                    pe.transpose(TR[:, QLR:QLR + C], c_n[t % 2], m.ident[:, :])
                    pe.wait_ge(krot_done, c * 8 + 2 * t + 2)
                    pe.transpose(KT[:, 0:P], k_rot[t % 2], m.ident[:, :]).then_inc(turned, 1)

                def fill(n):
                    kind, k = fills[n]
                    if n >= 3:
                        if fills[n - 3][0] == "turn":
                            pe.wait_ge(wot_copied, c * HG + fills[n - 3][1] + 1)
                        else:
                            pe.wait_ge(split_lo, c * SPLITS + split_of[n - 3] + 1)
                    out = fill_bank(n)
                    if kind == "nope":
                        if k == 0:
                            pe.wait_ge(nope_loaded, c * 16 + 16)
                            pe.wait_ge(kv_loaded, c * 16 + 16)
                        for h in range(HG):
                            mm = pe.matmul(out[:, h * C:h * C + C], nope[:, h, k * P:k * P + P],
                                           kv[:, h, 0, :], start=True, stop=True)
                    elif kind == "pe":
                        if k == 0:
                            pe.wait_ge(pe_loaded, c * 32 + 32)
                        for a in range(PAIRS):
                            mm = pe.transpose(out[:, a * P:a * P + P], pe_rows[:, a, k * P:k * P + P],
                                              m.ident[:, :])
                    elif kind == "turn":
                        if k == 0:
                            pe.wait_ge(wor_loaded, c * 16 + 16)
                        for o in range(KH):
                            mm = pe.transpose(out[:, o * P:o * P + P], wo_rows[:, o, k * DV:k * DV + DV],
                                              m.ident[:, :])
                    else:
                        pe.wait_ge(wot_copied, c * HG + k + 1)
                        mm = pe.matmul(out, kv[:, k, 1, :], wo_t[:, k, :], start=True, stop=True)
                    mm.then_inc(filled, 1)

                turn_x(0)
                for t in range(4):
                    project(t)
                    if t < 3:
                        turn_x(t + 1)
                    for n in beside[t]:
                        fill(n)
                    if t:
                        turn_results(t - 1)
                turn_results(3)
                pe.wait_ge(tok_lo, c * 12 + 12)
                pe.wait_ge(split_lo, c * SPLITS + SPLITS)

        def token_places(c, t):
            yield (TR[:, 0:QLR].rearrange("p (k n) -> p k n", k=KR), lambda a: m.cq[:, a, :, t * P:t * P + P], None)
            yield TR[:, QLR:QLR + C], lambda a: m.key_c[:, a, bass.ds(c * 512 + t * P, P)], kv_w
            yield KT[:, 0:P], lambda a: m.key_pe[:, a, bass.ds(c * 512 + t * P, P)], None

        @block.scalar
        def _(act):
            act.wait_ge(wa_turned, 1)
            for k in range(KH):
                nc.scalar.copy(wa_t[:, k, 0:QLR + C], m.bank[k]).then_inc(wa_copied, 1)
            nc.scalar.copy(wa_t[:, :, QLR + C:WA], m.bank[4][:, 0:KH * DR].rearrange("p (k n) -> p k n", k=KH)
                           ).then_inc(wa_copied, 1)
            act.wait_ge(consts_made, 4)
            with act.Fori(0, NCH) as c:
                def copy_x(t):
                    act.wait_ge(x_turned, c * 4 + t + 1)
                    nc.scalar.copy(x_t[t % 2], X).then_inc(xt_copied, 1)

                def hi(t):
                    if t == 0:
                        act.wait_ge(cq_free, c * 16 + 16)
                    act.wait_ge(turned, c * 4 + t + 1)
                    for src, dst, scale in token_places(c, t):
                        if scale is None:
                            nc.scalar.copy(dst(0), src).then_inc(tok_hi, 1)
                        else:
                            nc.scalar.activation(dst(0), src, ACT.Copy, scale=scale).then_inc(tok_hi, 1)

                copy_x(0)
                for t in range(4):
                    b = t % 2
                    act.wait_ge(proj_ready, c * 4 + t + 1)
                    nc.scalar.activation(squares[:, 0:QLR], PROJ[:, 0:QLR], ACT.Square, scale=QLR ** -0.5,
                                         accum_out=means[:, 2 * b:2 * b + 1]).then_inc(squared, 1)
                    nc.scalar.activation(squares[:, QLR:QLR + C], PROJ[:, QLR:QLR + C], ACT.Square, scale=C ** -0.5,
                                         accum_out=means[:, 2 * b + 1:2 * b + 2]).then_inc(squared, 1)
                    if t < 3:
                        copy_x(t + 1)
                    for n in beside[t]:
                        act.wait_ge(filled, c * FILLS + n + 1)
                        if fills[n][0] == "turn":
                            nc.scalar.copy(wo_t[:, fills[n][1], :], fill_bank(n)).then_inc(wot_copied, 1)
                        else:
                            if n == 0:
                                act.wait_ge(wq_free, c * 16 + 16)
                            elif fills[n] == ("out", 0):
                                act.wait_ge(wo_free, c * 16 + 16)
                            src, dst, scale = split_places(n)
                            nc.scalar.activation(dst(0), src, ACT.Copy, scale=scale).then_inc(split_hi, 1)
                    act.wait_ge(rstd_done, c * 4 + t + 1)
                    nc.scalar.activation(cq_n[b], PROJ[:, 0:QLR], ACT.Copy,
                                         scale=rstd[:, 2 * b:2 * b + 1]).then_inc(cqn_done, 1)
                    if t:
                        hi(t - 1)
                    if t == 2:
                        act.wait_ge(split_lo, c * SPLITS + WQ_SPLITS)
                        act.dma_start(m.wq_dram[c], words(m.wq)).then_inc(wq_free, 16)
                act.wait_ge(split_lo, c * SPLITS + SPLITS)
                act.dma_start(m.wo_dram[c], words(m.wo)).then_inc(wo_free, 16)
                hi(3)
                act.wait_ge(tok_lo, c * 12 + 12)
                act.dma_start(m.cq_dram[c], words(m.cq)).then_inc(cq_free, 16)
            for free in (wq_free, wo_free, cq_free):
                act.wait_ge(free, 16 * (NCH + 1))

        @block.vector
        def _(dve):
            nc.vector.memset(minus_half, -0.5).then_inc(consts_made, 1)
            dve.wait_ge(const_loaded, 16 * 3)
            nc.vector.tensor_copy(m.ident16[:, :], m.ident[:, :]).then_inc(consts_made, 1)
            dve.wait_ge(wq_free, 16)
            nc.vector.tensor_copy(m.mask16[:, :], mask).then_inc(consts_made, 1)
            nc.vector.tensor_scalar(q_w, q_w, SCALE, None, ALU.mult).then_inc(consts_made, 1)
            dve.wait_ge(consts_made, 4)
            dve.wait_ge(wo_free, 16)
            dve.wait_ge(cq_free, 16)
            with dve.Fori(0, NCH) as c:
                def lo(t):
                    for n, (src, dst, scale) in enumerate(token_places(c, t)):
                        dve.wait_ge(tok_hi, c * 12 + 3 * t + max(n, 1) + 1)
                        if scale is None:
                            nc.vector.tensor_tensor(dst(1), src, stored(dst(0)), ALU.subtract).then_inc(tok_lo, 1)
                        else:
                            nc.vector.scalar_tensor_tensor(out=dst(1), in0=src, scalar=scale, in1=stored(dst(0)),
                                                           op0=ALU.mult, op1=ALU.subtract).then_inc(tok_lo, 1)

                for t in range(4):
                    b = t % 2
                    tile = c * 4 + t
                    dve.wait_ge(proj_ready, tile + 1)
                    kp = KP[:, 0:DR].rearrange("p (a d) -> p a d", a=2)
                    cos_t = m.cos[:, bass.ds(tile, 1), :].broadcast_to([P, 2, HALF])
                    sin_t = m.sin[:, bass.ds(tile, 1), :]
                    tc = t_cos.rearrange("p (a d) -> p a d", a=2)
                    ts = t_sin.rearrange("p (a d) -> p a d", a=2)
                    nc.vector.tensor_tensor(tc, kp, cos_t, ALU.mult).then_inc(rope_parts, 1)
                    nc.vector.tensor_tensor(ts[:, 0:1], kp[:, 1:2], sin_t, ALU.mult).then_inc(rope_parts, 1)
                    nc.vector.tensor_tensor(ts[:, 1:2], kp[:, 0:1], sin_t, ALU.mult).then_inc(rope_parts, 1)
                    dve.wait_ge(rope_parts, c * 12 + 3 * t + 3)
                    kr = k_rot[b].rearrange("p (r a d) -> p r a d", r=2, a=2)
                    for a, op in ((0, ALU.subtract), (1, ALU.add)):
                        nc.vector.tensor_tensor(
                            kr[:, :, a, :], tc[:, a:a + 1, :].broadcast_to([P, 2, HALF]),
                            ts[:, a:a + 1, :].broadcast_to([P, 2, HALF]), op).then_inc(krot_done, 1)
                    dve.wait_ge(squared, c * 8 + 2 * t + 2)
                    nc.vector.tensor_scalar(safe[:, 2 * b:2 * b + 2], means[:, 2 * b:2 * b + 2], RMS_EPS, None,
                                            ALU.add).then_inc(eps_added, 1)
                    for n in beside[t]:
                        if fills[n][0] != "turn":
                            src, dst, scale = split_places(n)
                            dve.wait_ge(split_hi, c * SPLITS + split_of[n] + 1)
                            nc.vector.scalar_tensor_tensor(out=dst(1), in0=src, scalar=scale, in1=stored(dst(0)),
                                                           op0=ALU.mult, op1=ALU.subtract).then_inc(split_lo, 1)
                    dve.wait_ge(cqn_done, c * 4 + t + 1)
                    nc.vector.tensor_scalar(c_n[b], PROJ[:, QLR:QLR + C], rstd[:, 2 * b + 1:2 * b + 2],
                                            None, ALU.mult).then_inc(cn_done, 1)
                    dve.wait_ge(cn_done, c * 4 + t + 1)
                    v_hi = m.val[:, 0, bass.ds(tile, 1), :]
                    v_lo = m.val[:, 1, bass.ds(tile, 1), :]
                    cn3 = c_n[b].rearrange("p (a d) -> p a d", a=1)
                    nc.vector.tensor_copy(v_hi, cn3).then_inc(val_hi, 1)
                    dve.wait_ge(val_hi, c * 4 + t + 1)
                    nc.vector.tensor_tensor(v_lo, cn3, stored(v_hi), ALU.subtract)
                    if t:
                        lo(t - 1)
                lo(3)


def attention_phase(nc, m):
    with ExitStack() as ctx:
        def sb(name, shape, dt=F32):
            return ctx.enter_context(nc.sbuf_tensor(name, shape, dt))

        def sem(name):
            return ctx.enter_context(nc.semaphore(name))

        even = m.pool[:, 0:HG * (NT - 1) * P].rearrange("p (h k) -> p h k", h=HG)
        odd = m.pool[:, HG * (NT - 1) * P:].rearrange("p (h k) -> p h k", h=HG)
        probs = [even, odd]
        q_c = sb("q_c", [P, 2, HG, 512], F32R)
        q_pe = sb("q_pe", [P, HG, 512], F32R)
        turned_p = sb("turned_p", [P, 2, 2, 512], F32R)
        o_t = sb("o_t", [P, 2, 512], F32R)
        y = sb("y", [P, 2, HID])
        rot_cos = sb("rot_cos", [P, HG * DR])
        rot_sin = sb("rot_sin", [P, HG * DR])
        rot = sb("rot", [P, HG * P])
        half_max = m.small[:, 20:22]
        neg_max = m.small[:, 24:24 + HG]
        part_sum = m.small[:, 28:28 + 4 * HG]
        row_sum = m.small[:, 44:44 + HG]
        inv_sum = m.small[:, 48:48 + HG]
        TURN, OUT, MISC = [m.bank[4], m.bank[5]], m.bank[6], m.bank[7]

        wq_loaded = sem("wq_loaded")
        wo_loaded = sem("wo_loaded")
        cq_loaded = sem("cq_loaded")
        y_loaded = [sem(f"y_loaded{n}") for n in range(2)]
        y_stored = m.y_stored
        y_added = sem("y_added")
        scores_ready = sem("scores_ready")
        half_max_done = sem("half_max_done")
        max_done = sem("max_done")
        exp_done = sem("exp_done")
        sum_done = sem("sum_done")
        inv_done = sem("inv_done")
        norm_done = sem("norm_done")
        p_turned = sem("p_turned")
        p_hi = sem("p_hi")
        p_lo = sem("p_lo")
        pv_done = sem("pv_done")
        o_hi = sem("o_hi")
        o_lo = sem("o_lo")
        misc_ready = sem("misc_ready")
        q_hi = sem("q_hi")
        q_lo = sem("q_lo")
        rope_cos = sem("rope_cos")
        rope_sum = sem("rope_sum")
        rope_hi = sem("rope_hi")
        rope_lo = sem("rope_lo")
        qpe_done = sem("qpe_done")

        def banks(i):
            return (i + 4) // 4

        def width(i):
            return (i + 1) * P

        def place(i, h):
            return h % (4 // banks(i)) * banks(i)

        def halves(i):
            w = width(i)
            return [(0, w)] if banks(i) <= 2 else [(0, 1024), (1024, w)]

        def parts(i):
            w = width(i)
            return [(0, w)] if banks(i) <= 2 else [(c, min(c + 512, w)) for c in range(0, w, 512)]

        def score_count(i, h, b):
            return 4 * sum(banks(n) for n in range(i)) + h * banks(i) + b + 1

        def part_count(i, h, a):
            return 4 * sum(len(parts(n)) for n in range(i)) + h * len(parts(i)) + a + 1

        def two_part_count(i, h):
            return 4 * sum(len(parts(n)) > 1 for n in range(i)) + (h + 1)

        def head_count(i, h):
            return 4 * i + h + 1

        def key_count(i, j):
            return i * (i + 1) // 2 + j + 1

        SCORES, PARTS, HEADS, KEYS = score_count(NT, 0, -1), part_count(NT, 0, -1), 4 * NT, key_count(NT, -1)
        TWO = two_part_count(NT, -1)

        def quarter(i, h):
            n = i + 1
            return range(h * n // 4, (h + 1) * n // 4)

        def plan():
            for i in range(NT):
                for h in range(HG):
                    yield ("scores", i, h)
                    if h == 0 and i >= 1:
                        yield ("turn_probs", i - 1, 0)
                    if h == 0 and i >= 2:
                        yield ("y", i - 2)
                    if h == 1 and i + 1 < NT:
                        yield ("pe", i + 1)
                    if h == 3 and i + 1 < NT:
                        yield ("turn_pe", i + 1)
                    if i >= 1:
                        for j in quarter(i - 1, h):
                            yield ("work_off", i - 1, j)
                    yield ("normalise", i, h)
                    if i % 4 == 3 and i < NT - 1:
                        yield ("q", i // 4 + 1, h)
            between = {1: ("q", NCH, 0), 4: ("q", NCH, 1), 7: ("q", NCH, 2), 10: ("q", NCH, 3),
                       12: ("pe", NT), 14: ("turn_pe", NT)}
            yield ("turn_probs", NT - 1, 0)
            yield ("y", NT - 2)
            for j in range(NT):
                yield ("work_off", NT - 1, j)
                if j in between:
                    yield between[j]
            yield ("y", NT - 1)

        START = [("q", 0, h) for h in range(HG)] + [("pe", 0), ("turn_pe", 0)]
        uses = [u for u in plan() if u[0] in ("q", "pe", "turn_pe", "y")]
        use = {u: n for n, u in enumerate(uses)}
        USES = len(uses)

        def made(g, u):
            return START.index(u) + 1 if g is None else g * USES + len(START) + use[u] + 1

        def number(g, per_group, n):
            return n if g is None else g * per_group + n

        block = ctx.enter_context(nc.Block())

        @block.sync
        def _(sp):
            def load_cq(c):
                sp.dma_start(words(m.cq), m.cq_dram[c]
                             ).then_inc(cq_loaded, 16)

            def load_y(i):
                sp.dma_start(y[:, i % 2, :], m.y_dram[i]).then_inc(y_loaded[i % 2], 16)

            def store_y(g, i):
                sp.wait_ge(y_added, g * NT + i + 1)
                sp.dma_start(m.y_dram[i], y[:, i % 2, :]).then_inc(y_stored, 16)

            load_cq(0)
            with sp.Fori(0, G) as g:
                sp.dma_start(words(m.wo), m.wo_dram[g]
                             ).then_inc(wo_loaded, 16)
                for i in range(NT):
                    if i == 1:
                        sp.wait_ge(y_stored, g * (16 * NT) + 16)
                    if i >= 3:
                        sp.wait_ge(y_stored, g * (16 * NT) + 16 * (i - 1))
                    if i >= 1:
                        load_y(i - 1)
                    if i >= 2:
                        store_y(g, i - 2)
                    if i % 4 == 2:
                        sp.wait_ge(misc_ready, made(g, ("pe", i + 1)))
                        load_cq((i // 4 + 1) % NCH)
                sp.wait_ge(y_stored, g * (16 * NT) + 16 * (NT - 1))
                load_y(NT - 1)
                store_y(g, NT - 2)
                store_y(g, NT - 1)
            sp.wait_ge(y_stored, 16 * (NT * G + 1))
            sp.wait_ge(cq_loaded, 16 * (NCH * G + 1))

        @block.tensor
        def _(pe):
            def wait_read(g, u):
                if u[0] == "q":
                    pe.wait_ge(q_lo, number(g, NCH * HG, u[1] * HG + u[2] + 1))
                elif u[0] == "pe":
                    pe.wait_ge(rope_cos, number(g, 3 * NT, 3 * u[1] + 3))
                elif u[0] == "turn_pe":
                    pe.wait_ge(qpe_done, number(g, NT, u[1] + 1))
                else:
                    pe.wait_ge(y_added, number(g, NT, u[1] + 1))

            def shared(g, u):
                order = START if g is None else uses
                if order.index(u):
                    wait_read(g, order[order.index(u) - 1])

            def project_q(g, c, h):
                shared(g, ("q", c, h))
                if h == 0:
                    pe.wait_ge(cq_loaded, number(g, 16 * NCH, 16 * (c + 1)))
                    if c % NCH == 0:
                        pe.wait_ge(wq_loaded, 16 if g is None else g * 16 + 32)
                n = 0
                for k in range(KR):
                    for a, b in ((0, 0), (1, 0), (0, 1)):
                        mm = pe.matmul(MISC, m.wq[:, a, k, h * C:h * C + C], m.cq[:, b, k, :],
                                       start=(n == 0), stop=(n == 3 * KR - 1))
                        n += 1
                mm.then_inc(misc_ready, 1)

            def project_pe(g, t):
                shared(g, ("pe", t))
                n = 0
                for k in range(KR):
                    for a, b in ((0, 0), (1, 0), (0, 1)):
                        mm = pe.matmul(MISC[:, 0:HG * DR], m.cq[:, a, k, t % 4 * P:t % 4 * P + P],
                                       m.wq[:, b, k, HG * C:WCOL], start=(n == 0), stop=(n == 3 * KR - 1))
                        n += 1
                mm.then_inc(misc_ready, 1)

            def turn_pe(g, t):
                shared(g, ("turn_pe", t))
                pe.wait_ge(rope_lo, number(g, NT, t + 1))
                for h in range(HG):
                    mm = pe.transpose(MISC[:, h * P:h * P + P], rot[:, h * P:h * P + P], m.ident[:, :])
                mm.then_inc(misc_ready, 1)

            for h in range(HG):
                project_q(None, 0, h)
            project_pe(None, 0)
            turn_pe(None, 0)
            wait_read(None, START[-1])
            with pe.Fori(0, G) as g:
                def read_before(i, h, b):
                    bank = place(i, h) + b
                    for n in range(4 * i + h - 1, -1, -1):
                        pi, ph = n // 4, n % 4
                        at = bank - place(pi, ph)
                        if 0 <= at < banks(pi):
                            return part_count(pi, ph, at if len(parts(pi)) > 1 else 0)
                    return 0

                def scores(i, h):
                    t = i % 4 * P
                    if h == 0:
                        if i % 4 == 0:
                            pe.wait_ge(q_lo, g * (NCH * HG) + (i // 4) * HG + HG)
                        pe.wait_ge(qpe_done, g * NT + i + 1)
                    for b in range(banks(i)):
                        before = read_before(i, h, b)
                        if before:
                            pe.wait_ge(exp_done, g * PARTS + before)
                        k0 = b * 512
                        n_k = min(512, width(i) - k0)
                        diagonal = b == banks(i) - 1
                        out = m.bank[place(i, h) + b]
                        row = out[:, 0:n_k]
                        terms = [(q_c[:, 0, h, t:t + P], m.key_c[:, 0, k0:k0 + n_k]),
                                 (q_c[:, 0, h, t:t + P], m.key_c[:, 1, k0:k0 + n_k]),
                                 (q_c[:, 1, h, t:t + P], m.key_c[:, 0, k0:k0 + n_k]),
                                 (q_pe[:, h, t:t + P], m.key_pe[:, 0, k0:k0 + n_k]),
                                 (q_pe[:, h, t:t + P], m.key_pe[:, 1, k0:k0 + n_k])]
                        for x, (q, k) in enumerate(terms):
                            mm = pe.matmul(row, q, k, start=(x == 0), stop=(x == 4 and not diagonal))
                        if diagonal:
                            mm = pe.matmul(row[:, n_k - P:n_k], m.ident16[:, :], m.mask16[:, :],
                                           start=False, stop=True)
                        mm.then_inc(scores_ready, 1)

                def turn_probs(i, j):
                    if j == 0:
                        pe.wait_ge(norm_done, g * HEADS + head_count(i, HG - 1))
                    n = key_count(i, j)
                    if n > 2:
                        pe.wait_ge(p_lo, g * KEYS + n - 2)
                    for h in range(HG):
                        mm = pe.transpose(TURN[n % 2][:, h * P:h * P + P], probs[i % 2][:, h, j * P:j * P + P],
                                          m.ident[:, :])
                    mm.then_inc(p_turned, 1)

                def values_hi(i, j):
                    if j == 0 and i > 0:
                        pe.wait_ge(o_lo, g * NT + i)
                    n = key_count(i, j)
                    pe.wait_ge(p_hi, g * KEYS + n)
                    pe.matmul(OUT, m.val[:, 0, j, :], turned_p[:, n % 2, 0, :], start=(j == 0), stop=False)
                    pe.matmul(OUT, m.val[:, 1, j, :], turned_p[:, n % 2, 0, :], start=False, stop=False)

                def values_lo(i, j):
                    n = key_count(i, j)
                    pe.wait_ge(p_lo, g * KEYS + n)
                    pe.matmul(OUT, m.val[:, 0, j, :], turned_p[:, n % 2, 1, :], start=False,
                              stop=(j == i)).then_inc(pv_done, 1)

                def work_off(i, j):
                    if j < i:
                        turn_probs(i, j + 1)
                    values_hi(i, j)
                    if j >= 1:
                        values_lo(i, j - 1)
                    if j == i:
                        values_lo(i, j)

                def project_out(i):
                    shared(g, ("y", i))
                    if i == 0:
                        pe.wait_ge(wo_loaded, g * 16 + 16)
                    pe.wait_ge(o_lo, g * NT + i + 1)
                    n = 0
                    for h in range(HG):
                        for a, b in ((0, 0), (0, 1), (1, 0)):
                            mm = pe.matmul(MISC, o_t[:, a, h * P:h * P + P], m.wo[:, b, h, :],
                                           start=(n == 0), stop=(n == 3 * HG - 1))
                            n += 1
                    mm.then_inc(misc_ready, 1)

                for what, *at in plan():
                    if what == "scores":
                        scores(*at)
                    elif what == "turn_probs":
                        turn_probs(*at)
                    elif what == "work_off":
                        work_off(*at)
                    elif what == "q":
                        project_q(g, *at)
                    elif what == "pe":
                        project_pe(g, *at)
                    elif what == "turn_pe":
                        turn_pe(g, *at)
                    elif what == "y":
                        project_out(*at)
                wait_read(g, uses[-1])

        @block.scalar
        def _(act):
            def other(g, u):
                if u[0] == "q":
                    act.wait_ge(misc_ready, made(g, u))
                    nc.scalar.copy(q_c[:, 0, u[2], :], MISC).then_inc(q_hi, 1)
                elif u[0] == "pe":
                    act.wait_ge(rope_sum, number(g, 2 * NT, 2 * u[1] + 2))
                    nc.scalar.copy(rot[:, :].bitcast(F32R).rearrange("p (h a d) -> p h a d", h=HG, a=2)[:, :, 0, :],
                                   rot_cos[:, :].rearrange("p (h d) -> p h d", h=HG)).then_inc(rope_hi, 1)
                elif u[0] == "turn_pe":
                    t = u[1] % 4 * P
                    act.wait_ge(misc_ready, made(g, u))
                    nc.scalar.copy(q_pe[:, :, t:t + P], MISC.rearrange("p (h n) -> p h n", h=HG)).then_inc(qpe_done, 1)

            for u in START:
                other(None, u)
            with act.Fori(0, G) as g:
                def hi(i, j):
                    n = key_count(i, j)
                    act.wait_ge(p_turned, g * KEYS + n)
                    nc.scalar.copy(turned_p[:, n % 2, 0, :], TURN[n % 2]).then_inc(p_hi, 1)

                def exp(i, h, a):
                    c0, c1 = parts(i)[a]
                    act.wait_ge(max_done, g * HEADS + head_count(i, h))
                    row = m.rows[:, place(i, h) * 512 + c0:place(i, h) * 512 + c1]
                    nc.scalar.activation(probs[i % 2][:, h, c0:c1], row, ACT.Exp, bias=neg_max[:, h:h + 1],
                                         accum_out=part_sum[:, 4 * h + a:4 * h + a + 1]).then_inc(exp_done, 1)

                due = []
                for what, *at in plan():
                    if what == "scores":
                        due = [(*at, a) for a in range(len(parts(at[0])))]
                    elif what == "turn_probs":
                        hi(*at)
                    elif what == "work_off":
                        i, j = at
                        if j < i:
                            hi(i, j + 1)
                        if due:
                            exp(*due.pop(0))
                        if j == i:
                            act.wait_ge(pv_done, g * KEYS + key_count(i, i))
                            nc.scalar.copy(o_t[:, 0, :], OUT).then_inc(o_hi, 1)
                    elif what == "normalise":
                        for x in due:
                            exp(*x)
                        due = []
                    else:
                        other(g, (what, *at))

        @block.gpsimd
        def _(pool):
            hi = rot[:, :].rearrange("p (h a d) -> p h a d", h=HG, a=2)[:, :, 0, :]
            lo = rot[:, :].rearrange("p (h a d) -> p h a d", h=HG, a=2)[:, :, 1, :]
            ca = rot_cos[:, :].rearrange("p (h a d) -> p h a d", h=HG, a=2)
            sa = rot_sin[:, :].rearrange("p (h a d) -> p h a d", h=HG, a=2)
            def rotate(n):
                pool.wait_ge(rope_cos, n * 3 + 3)
                nc.gpsimd.tensor_tensor(ca[:, :, 0, :], ca[:, :, 0, :], sa[:, :, 0, :], ALU.subtract
                                        ).then_inc(rope_sum, 1)
                nc.gpsimd.tensor_tensor(ca[:, :, 1, :], ca[:, :, 1, :], sa[:, :, 1, :], ALU.add
                                        ).then_inc(rope_sum, 1)
                pool.wait_ge(rope_hi, n + 1)
                nc.gpsimd.tensor_tensor(lo, rot_cos[:, :].rearrange("p (h d) -> p h d", h=HG), hi,
                                        ALU.subtract).then_inc(rope_lo, 1)

            pool.dma_start(words(m.wq), m.wq_dram[0]).then_inc(wq_loaded, 16)
            rotate(0)
            with pool.Fori(0, G) as g:
                with pool.Fori(1, NT) as t:
                    rotate(g * NT + t)
                pool.wait_ge(misc_ready, made(g, ("pe", NT - 1)))
                pool.dma_start(words(m.wq), m.wq_dram[(g + 1) % G]).then_inc(wq_loaded, 16)
                rotate(g * NT + NT)

        @block.vector
        def _(dve):
            def other(g, u):
                if u[0] == "q":
                    _, c, h = u
                    dve.wait_ge(q_hi, number(g, NCH * HG, c * HG + h + 1))
                    nc.vector.tensor_tensor(q_c[:, 1, h, :], MISC, stored(q_c[:, 0, h, :]), ALU.subtract
                                            ).then_inc(q_lo, 1)
                elif u[0] == "pe":
                    t = u[1] % NT
                    dve.wait_ge(misc_ready, made(g, u))
                    q = MISC[:, 0:HG * DR].rearrange("p (h a d) -> p h a d", h=HG, a=2)
                    ca = rot_cos[:, :].rearrange("p (h d) -> p h d", d=HALF)
                    sa = rot_sin[:, :].rearrange("p (h a d) -> p h a d", h=HG, a=2)
                    cos_t = m.cos[:, t:t + 1, :].broadcast_to([P, 2 * HG, HALF])
                    sin_t = m.sin[:, t:t + 1, :].broadcast_to([P, HG, HALF])
                    nc.vector.tensor_tensor(ca, MISC[:, 0:HG * DR].rearrange("p (h d) -> p h d", d=HALF), cos_t,
                                            ALU.mult).then_inc(rope_cos, 1)
                    nc.vector.tensor_tensor(sa[:, :, 0, :], q[:, :, 1, :], sin_t, ALU.mult).then_inc(rope_cos, 1)
                    nc.vector.tensor_tensor(sa[:, :, 1, :], q[:, :, 0, :], sin_t, ALU.mult).then_inc(rope_cos, 1)
                elif u[0] == "y":
                    i = u[1]
                    dve.wait_ge(misc_ready, made(g, u))
                    dve.wait_ge(y_loaded[i % 2], g * (8 * NT) + 16 * (i // 2 + 1))
                    nc.vector.tensor_tensor(y[:, i % 2, :], MISC, y[:, i % 2, :], ALU.add).then_inc(y_added, 1)

            for u in START:
                other(None, u)
            with dve.Fori(0, G) as g:
                def lo(i, j):
                    n = key_count(i, j)
                    dve.wait_ge(p_hi, g * KEYS + n)
                    if n > 2:
                        dve.wait_ge(pv_done, g * KEYS + n - 2)
                    nc.vector.tensor_tensor(turned_p[:, n % 2, 1, :], TURN[n % 2], stored(turned_p[:, n % 2, 0, :]),
                                            ALU.subtract).then_inc(p_lo, 1)

                def maxima(i, h):
                    first = place(i, h) * 512
                    for a, (c0, c1) in enumerate(halves(i)):
                        dve.wait_ge(scores_ready, g * SCORES + score_count(i, h, (c1 - 1) // 512))
                        row = m.rows[:, first + c0:first + c1]
                        if len(halves(i)) == 1:
                            nc.vector.tensor_reduce(neg_max[:, h:h + 1], row, AX.X, ALU.max, negate=True
                                                    ).then_inc(max_done, 1)
                        else:
                            nc.vector.tensor_reduce(half_max[:, a:a + 1], row, AX.X, ALU.max
                                                    ).then_inc(half_max_done, 1)
                    if len(halves(i)) == 2:
                        dve.wait_ge(half_max_done, g * (2 * TWO) + 2 * two_part_count(i, h))
                        nc.vector.tensor_reduce(neg_max[:, h:h + 1], half_max, AX.X, ALU.max, negate=True
                                                ).then_inc(max_done, 1)

                def normalise(i, h):
                    n_parts = len(parts(i))
                    dve.wait_ge(exp_done, g * PARTS + part_count(i, h, n_parts - 1))
                    total = part_sum[:, 4 * h:4 * h + 1]
                    if n_parts > 1:
                        total = row_sum[:, h:h + 1]
                        nc.vector.tensor_reduce(total, part_sum[:, 4 * h:4 * h + n_parts], AX.X, ALU.add
                                                ).then_inc(sum_done, 1)
                        dve.wait_ge(sum_done, g * TWO + two_part_count(i, h))
                    nc.vector.reciprocal(inv_sum[:, h:h + 1], total).then_inc(inv_done, 1)
                    dve.wait_ge(inv_done, g * HEADS + head_count(i, h))
                    p = probs[i % 2][:, h, 0:width(i)]
                    nc.vector.tensor_scalar(p, p, inv_sum[:, h:h + 1], None, ALU.mult).then_inc(norm_done, 1)

                for what, *at in plan():
                    if what == "scores":
                        maxima(*at)
                    elif what == "turn_probs":
                        lo(*at)
                    elif what == "work_off":
                        i, j = at
                        if j < i:
                            lo(i, j + 1)
                        else:
                            dve.wait_ge(o_hi, g * NT + i + 1)
                            nc.vector.tensor_tensor(o_t[:, 1, :], OUT, stored(o_t[:, 0, :]), ALU.subtract
                                                    ).then_inc(o_lo, 1)
                    elif what == "normalise":
                        normalise(*at)
                    else:
                        other(g, (what, *at))


def ffn_phase(nc, m, w, scale_w, bias, out):
    with ExitStack() as ctx:
        def sem(name):
            return ctx.enter_context(nc.semaphore(name))

        at = 0

        def stage(n):
            nonlocal at
            at += n
            return m.pool[:, at - n:at]

        def sb(name, n):
            return ctx.enter_context(nc.sbuf_tensor(name, [P, n], F32))[:, :]

        y_all = stage(NT * HID).rearrange("p (t d) -> p t d", t=NT)
        w_rows = stage(KH * HID).rearrange("p (o i) -> p o i", o=KH)
        w_s = stage(KH * HID).rearrange("p (o i) -> p o i", o=KH)
        w_t = sb("w_t", KH * HID).rearrange("p (k o) -> p k o", k=KH)
        bias_rows = sb("bias_rows", HID)
        x1 = [sb(f"x1_{b}", HID) for b in range(2)]
        x1b = [sb(f"x1b_{b}", HID) for b in range(2)]
        x1_t = [sb(f"x1t_{b}", HID) for b in range(2)]
        z = [sb(f"z_{b}", HID) for b in range(2)]
        o_out = [sb(f"o_out{b}", HID) for b in range(2)]
        w_scale = m.small[:, 0:4]
        minus_half = m.small[:, 4:5]
        spare = m.small[:, 5:6]
        epsilon = m.small[:, 6:7]
        stats = [m.small[:, 8 + 6 * b:14 + 6 * b] for b in range(4)]
        agg = [m.small[:, 32 + 2 * b:34 + 2 * b] for b in range(4)]
        safe = [m.small[:, 40 + b:41 + b] for b in range(4)]
        inv = [m.small[:, 44 + b:45 + b] for b in range(4)]

        w_loaded = sem("ffn_w_loaded")
        y_first_loaded = sem("y_first_loaded")
        y_rest_loaded = sem("y_rest_loaded")
        w_scaled = sem("ffn_w_scaled")
        w_turned = sem("ffn_w_turned")
        w_copied = sem("ffn_w_copied")
        half_set = sem("half_set")
        bn_done = sem("bn_done")
        aggr_done = sem("aggr_done")
        ln_eps_added = sem("ln_eps_added")
        inv_ready = sem("inv_ready")
        x1_done = sem("x1_done")
        x1b_done = sem("x1b_done")
        x1_turned = sem("x1_turned")
        x1t_copied = sem("x1t_copied")
        lin_ready = sem("lin_ready")
        z_done = sem("z_done")
        out_done = sem("out_done")
        out_free = [sem(f"out_free{n}") for n in range(2)]

        block = ctx.enter_context(nc.Block())
        out_v = out.rearrange("(t p) d -> t p d", p=P)
        LAST = NT - 1

        def turns(eng, tile):
            with eng.Fori(0, NT // 2 - 1) as n:
                tile(n * 2, 0, 2)
                tile(n * 2 + 1, 1, 2)
            tile(LAST - 1, 0, 1)
            tile(LAST, 1, 0)

        def y_number(u, after):
            return u * 2 + 2

        def z_number(u, after):
            return u * 2 + (3 if after == 2 else 2 if after == 1 else 1)

        @block.sync
        def _(sp):
            y_v = m.y_dram.rearrange("t p d -> p t d")
            sp.dma_start(y_all[:, 0:2, :], y_v[:, 0:2, :]).then_inc(y_first_loaded, 16)
            sp.dma_start(w_rows, w.rearrange("(o p) i -> p o i", p=P)).then_inc(w_loaded, 16)
            sp.dma_start(w_scale, scale_w.rearrange("(o p) -> p o", p=P),
                         allow_slow_non_contiguous=True).then_inc(w_loaded, 16)
            sp.dma_start(bias_rows[:, 0:HID // 2], bias.rearrange("(a d) -> a d", a=1)[:, 0:HID // 2]
                         .broadcast_to([P, HID // 2])).then_inc(out_free[0], 16)
            sp.dma_start(bias_rows[:, HID // 2:HID], bias.rearrange("(a d) -> a d", a=1)[:, HID // 2:HID]
                         .broadcast_to([P, HID // 2])).then_inc(out_free[1], 16)
            sp.dma_start(y_all[:, 2:NT, :], y_v[:, 2:NT, :]).then_inc(y_rest_loaded, 16)

        @block.gpsimd
        def _(pool):
            def invert(b, idx):
                pool.wait_ge(aggr_done, idx + 1)
                nc.gpsimd.tensor_tensor(safe[b], agg[b][:, 1:2], epsilon, ALU.add).then_inc(ln_eps_added, 1)
                pool.wait_ge(ln_eps_added, idx + 1)
                nc.gpsimd.tensor_tensor(inv[b], safe[b], minus_half, ALU.pow).then_inc(inv_ready, 1)

            def add_bias(u, b):
                pool.wait_ge(x1_done, u + 1)
                nc.gpsimd.tensor_tensor(x1b[b], x1[b], bias_rows, ALU.add).then_inc(x1b_done, 1)

            def tile(u, b, after):
                if after:
                    add_bias(u + 1, 1 - b)
                if after == 2:
                    invert(b, y_number(u, after))
                invert(2 + b, z_number(u, after))

            for b in range(2):
                pool.wait_ge(out_free[b], 16)
            pool.wait_ge(half_set, 2)
            invert(0, 0)
            invert(1, 1)
            add_bias(0, 0)
            turns(pool, tile)

        @block.tensor
        def _(pe):
            pe.wait_ge(w_scaled, KH)
            for k in range(KH):
                for o in range(KH):
                    mm = pe.transpose(m.bank[4 + k][:, o * P:o * P + P], w_s[:, o, k * P:k * P + P], m.ident[:, :])
                mm.then_inc(w_turned, 1)

            def turn_x1(u, b):
                pe.wait_ge(x1_done, u + 1)
                for k in range(KH):
                    mm = pe.transpose(m.bank[b][:, k * P:k * P + P], x1[b][:, k * P:k * P + P], m.ident[:, :])
                mm.then_inc(x1_turned, 1)

            def linear(u, b):
                pe.wait_ge(x1t_copied, u + 1)
                for k in range(KH):
                    mm = pe.matmul(m.bank[2 + b], x1_t[b][:, k * P:k * P + P], w_t[:, k, :],
                                   start=(k == 0), stop=(k == KH - 1))
                mm.then_inc(lin_ready, 1)

            def tile(u, b, after):
                linear(u, b)
                if after:
                    turn_x1(u + 1, 1 - b)

            turn_x1(0, 0)
            pe.wait_ge(w_copied, KH)
            turns(pe, tile)

        @block.scalar
        def _(act):
            act.wait_ge(w_loaded, 32)
            for o in range(KH):
                nc.scalar.activation(w_s[:, o, :], w_rows[:, o, :], ACT.Copy, scale=w_scale[:, o:o + 1]
                                     ).then_inc(w_scaled, 1)
            for k in range(KH):
                act.wait_ge(w_turned, k + 1)
                nc.scalar.copy(w_t[:, k, :], m.bank[4 + k]).then_inc(w_copied, 1)

            def copy_x1(u, b):
                act.wait_ge(x1_turned, u + 1)
                nc.scalar.copy(x1_t[b], m.bank[b]).then_inc(x1t_copied, 1)

            def tile(u, b, after):
                if after:
                    copy_x1(u + 1, 1 - b)
                act.wait_ge(out_done, u + 1)
                act.dma_start(out_v[u], o_out[b]).then_inc(out_free[b], 16)

            copy_x1(0, 0)
            turns(act, tile)
            for b in range(2):
                act.wait_ge(out_free[b], 16 * (NT // 2 + 1))

        @block.vector
        def _(dve):
            nc.vector.memset(minus_half, -0.5).then_inc(half_set, 1)

            nc.vector.memset(epsilon, LN_EPS).then_inc(half_set, 1)

            def statistics(src, slot, number):
                nc.vector.bn_stats(stats[slot], src).then_inc(bn_done, 1)
                dve.wait_ge(bn_done, number + 1)
                nc.vector.memset(spare, 0.0)
                nc.vector.bn_aggr(agg[slot], stats[slot]).then_inc(aggr_done, 1)

            def apply(src, dst, slot, number, done):
                dve.wait_ge(inv_ready, number + 1)
                nc.vector.tensor_scalar(dst, src, agg[slot][:, 0:1], inv[slot], ALU.subtract, ALU.mult
                                        ).then_inc(done, 1)

            def y_tile(u):
                return y_all[:, bass.ds(u, 1), :].rearrange("p a d -> p (a d)")

            def tile(u, b, after):
                if after:
                    nc.vector.tensor_scalar(x1[1 - b], y_tile(u + 1), agg[1 - b][:, 0:1], inv[1 - b],
                                            ALU.subtract, ALU.mult).then_inc(x1_done, 1)
                if after == 2:
                    statistics(y_tile(u + 2), b, y_number(u, after))
                dve.wait_ge(lin_ready, u + 1)
                dve.wait_ge(x1b_done, u + 1)
                nc.vector.tensor_tensor(z[b], m.bank[2 + b], x1b[b], ALU.add).then_inc(z_done, 1)
                dve.wait_ge(z_done, u + 1)
                statistics(z[b], 2 + b, z_number(u, after))
                dve.wait_ge(out_free[b], (u - b) * 8 + 16)
                apply(z[b], o_out[b], 2 + b, z_number(u, after), out_done)

            dve.wait_ge(y_first_loaded, 16)
            statistics(y_tile(0), 0, 0)
            statistics(y_tile(1), 1, 1)
            apply(y_tile(0), x1[0], 0, 1, x1_done)
            dve.wait_ge(y_rest_loaded, 16)
            turns(dve, tile)


def build(nc, x, w_qa, q_ln, w_qb, w_kva, kv_ln, w_kvb, w_o, ffn_w, ffn_scale, ffn_bias,
          ident_in, mask_in, cos_in, sin_in, out):
    with ExitStack() as ctx:
        m = Memory(nc, ctx)
        x2, out2 = x[0], out[0]
        prepare_phase(nc, m, x2, w_qa, w_kva, w_qb, w_kvb, w_o, q_ln, kv_ln, ident_in, mask_in, cos_in, sin_in)
        attention_phase(nc, m)
        ffn_phase(nc, m, ffn_w, ffn_scale, ffn_bias, out2)


_INS = ['L0_attn_hidden_states', 'L0_attn_w_qa', 'L0_attn_q_a_ln_w', 'L0_attn_w_qb', 'L0_attn_w_kva',
        'L0_attn_kv_a_ln_w', 'L0_attn_w_kvb', 'L0_attn_w_o', 'L0_ffn_weight', 'L0_ffn_scale_weight',
        'L0_ffn_bias']


def _constants():
    inv_freq = (1.0 / np.float32(10000.0) ** (np.arange(0, DR, 2, dtype=np.float32) / np.float32(DR))).astype(np.float32)
    angle = np.outer(np.arange(S, dtype=np.float32), inv_freq).astype(np.float32)
    return {
        "ident": np.eye(P, dtype=np.float32),
        "mask": np.triu(np.full((P, P), MASKED, np.float32), k=1),
        "cos": np.cos(angle).astype(np.float32),
        "sin": np.sin(angle).astype(np.float32),
    }


def kernel(**inputs):
    import numpy as _np
    import concourse.bacc as _bacc
    from concourse import mybir as _mybir
    from concourse.bass_utils import run_bass_kernel_spmd as _run

    nc = _bacc.Bacc("TRN2", target_bir_lowering=False, num_devices=1)
    arrays, args = {}, []
    named = {f"in_{n}": _np.ascontiguousarray(inputs[n]) for n in _INS}
    named.update({f"const_{n}": a for n, a in _constants().items()})
    for name, a in named.items():
        arrays[name] = a
        args.append(nc.dram_tensor(name, a.shape, _mybir.dt.from_np(a.dtype), kind="ExternalInput").ap())
    out = nc.dram_tensor("out_dram", (1, S, HID), _mybir.dt.float32, kind="ExternalOutput").ap()
    build(nc, *args, out)
    r = _run(nc, [arrays], core_ids=[0])
    return r.results[0]["out_dram"]
```

```python
from contextlib import ExitStack

import numpy as np

import concourse.bass as bass
from concourse import mybir

F32 = mybir.dt.float32
F32R = mybir.dt.float32r
BF16 = mybir.dt.bfloat16
ALU = mybir.AluOpType
ACT = mybir.ActivationFunctionType
AX = mybir.AxisListType

P = 128
S = 2048
HID = 512
H = 16
QLR = 384
C = 128
DN, DR, DV = 128, 64, 128
DQ = DN + DR
HALF = DR // 2
SCALE = DQ ** -0.5
RMS_EPS, LN_EPS = 1e-6, 1e-5
MASKED = -1e38

NT = S // P
NCH = NT // 4
G = 4
HG = H // G
KR = QLR // P
KH = HID // P
WCOL = HG * C + HG * DR
PAIRS = HG // 2


def chunk(c):
    return (c + 1) % NCH


def stored(view):
    return view.bitcast(F32)


def words(buffer):
    return stored(buffer[:, :, :, :].rearrange("p a k n -> p (a k n)"))


class Memory:

    def __init__(self, nc, ctx):
        def sb(name, shape, dt=F32):
            return ctx.enter_context(nc.sbuf_tensor(name, shape, dt))

        self.bank = [ctx.enter_context(nc.psum_tensor(f"bank{n}", [P, 512], F32)) for n in range(4, 8)]
        self.rows = ctx.enter_context(nc.psum_tensor("rows", [P, 4 * 512], F32))
        self.bank = [self.rows[:, 512 * n:512 * n + 512] for n in range(4)] + [b[:, :] for b in self.bank]

        self.key_c = sb("key_c", [P, 2, S], F32R)
        self.key_pe = sb("key_pe", [P, 2, S], F32R)
        self.val = sb("val", [P, 2, NT, C], F32R)
        self.cq = sb("cq", [P, 2, KR, 512], F32R)
        self.wq = sb("wq", [P, 2, KR, WCOL], F32R)
        self.wo = sb("wo", [P, 2, HG, HID], F32R)
        self.ident = sb("ident", [P, P])
        self.ident16 = sb("ident16", [P, P], BF16)
        self.mask16 = sb("mask16", [P, P], BF16)
        self.cos = sb("cos", [P, NT, HALF])
        self.sin = sb("sin", [P, NT, HALF])
        self.small = sb("small", [P, 64])
        self.pool = sb("pool", [P, HG * (NT - 1) * P + HG * NT * P])

        self.cq_dram = nc.dram_tensor("cq_dram", (NCH, P, 2 * KR * 512), F32, kind="Internal").ap()
        self.wq_dram = nc.dram_tensor("wq_dram", (G, P, 2 * KR * WCOL), F32, kind="Internal").ap()
        self.wo_dram = nc.dram_tensor("wo_dram", (G, P, 2 * HG * HID), F32, kind="Internal").ap()
        self.y_stored = ctx.enter_context(nc.semaphore("y_stored"))
        self.wo_free = ctx.enter_context(nc.semaphore("wo_free"))
        self.cq_free = ctx.enter_context(nc.semaphore("cq_free"))
        self.ffn_w_loaded = ctx.enter_context(nc.semaphore("ffn_w_loaded"))
        self.y_first_loaded = ctx.enter_context(nc.semaphore("y_first_loaded"))
        self.y_dram = nc.dram_tensor("y_dram", (NT, P, HID), F32, kind="Internal").ap()


def prepare_phase(nc, m, x, w_qa, w_kva, w_qb, w_kvb, w_o, q_ln, kv_ln, ident_in, mask_in, cos_in, sin_in):
    with ExitStack() as ctx:
        def sem(name):
            return ctx.enter_context(nc.semaphore(name))

        at = 0

        def stage(n):
            nonlocal at
            at += n
            return m.pool[:, at - n:at]

        def sb(name, n):
            return ctx.enter_context(nc.sbuf_tensor(name, [P, n], F32))[:, :]

        WA = QLR + C + DR
        nope = stage(HG * QLR).rearrange("p (h r) -> p h r", h=HG)
        pe_rows = stage(PAIRS * QLR).rearrange("p (a r) -> p a r", a=PAIRS)
        kv = stage(HG * 2 * C).rearrange("p (h k c) -> p h k c", h=HG, k=2)
        wo_rows = stage(KH * HG * DV).rearrange("p (o d) -> p o d", o=KH)
        wo_t = stage(HG * HID).rearrange("p (h o) -> p h o", h=HG)
        mask = stage(P)
        wa_t = stage(KH * WA).rearrange("p (k n) -> p k n", k=KH)
        x_in = stage(4 * HID).rearrange("p (t i) -> p t i", t=4)
        x_t = [stage(HID) for _ in range(2)]
        cq_n = [stage(QLR) for _ in range(2)]
        wa_rows = sb("wa_rows", 4 * HID).rearrange("p (o i) -> p o i", o=4)
        wa_tail = sb("wa_tail", HID)
        squares = sb("squares", QLR + C)
        c_n = [sb(f"c_n{b}", C) for b in range(2)]
        k_rot = [sb(f"k_rot{b}", P) for b in range(2)]
        t_cos = sb("t_cos", DR)
        t_sin = sb("t_sin", DR)
        q_w = m.small[:, 0:KR]
        kv_w = m.small[:, 4:5]
        minus_half = m.small[:, 6:8]
        means = m.small[:, 8:12]
        safe = m.small[:, 12:16]
        rstd = m.small[:, 16:20]

        const_loaded = sem("const_loaded")
        consts_made = sem("consts_made")
        wa_loaded = sem("wa_loaded")
        wa_turned = sem("wa_turned")
        wa_copied = sem("wa_copied")
        x_loaded = [sem(f"x_loaded{t}") for t in range(4)]
        x_turned = sem("x_turned")
        xt_copied = sem("xt_copied")
        proj_ready = sem("proj_ready")
        squared = sem("squared")
        eps_added = sem("eps_added")
        rstd_done = sem("rstd_done")
        cqn_done = sem("cqn_done")
        cn_done = sem("cn_done")
        val_hi = sem("val_hi")
        rope_parts = sem("rope_parts")
        krot_done = sem("krot_done")
        turned = sem("turned")
        tok_hi = sem("tok_hi")
        tok_lo = sem("tok_lo")
        nope_loaded = sem("nope_loaded")
        pe_loaded = sem("pe_loaded")
        kv_loaded = [sem(f"kv_loaded{k}") for k in range(2)]
        wor_loaded = sem("wor_loaded")
        filled = sem("filled")
        wot_copied = sem("wot_copied")
        split_hi = sem("split_hi")
        split_lo = sem("split_lo")
        wq_free = sem("wq_free")
        wo_free, cq_free = m.wo_free, m.cq_free

        X, PROJ, TR = m.bank[0], m.bank[1:3], m.bank[3]
        KP, KT = m.bank[4][:, 0:DR], m.bank[4][:, P:2 * P]

        fills = [("nope", k) for k in range(KR)] + [("pe", k) for k in range(KR)] \
            + [("turn", h) for h in range(HG)] + [("out", h) for h in range(HG)]
        beside = [range(0, 3), range(3, 7), range(7, 10), range(10, 12)]
        at_end = range(12, 14)
        FILLS = len(fills)
        split_of = {n: s for s, n in enumerate(n for n, f in enumerate(fills) if f[0] != "turn")}
        SPLITS = len(split_of)
        WQ_SPLITS = 2 * KR
        TOK = 12

        def fill_bank(n):
            return m.bank[5 + n % 3]

        def last_in_bank(n):
            return max(f for f in range(FILLS) if f % 3 == n % 3)

        def split_places(n):
            kind, k = fills[n]
            if kind == "nope":
                return fill_bank(n), lambda a: m.wq[:, a, k, 0:HG * C], q_w[:, k:k + 1]
            if kind == "pe":
                return fill_bank(n)[:, 0:HG * DR], lambda a: m.wq[:, a, k, HG * C:WCOL], q_w[:, k:k + 1]
            return fill_bank(n), lambda a: m.wo[:, a, k, :], kv_w

        wqb_v = w_qb.rearrange("(g h q) r -> g q h r", g=G, h=HG)
        wpe_v = w_qb.rearrange("(g a e q) r -> g e q a r", g=G, a=PAIRS, e=2)
        kvb_v = w_kvb.rearrange("(g h k d) c -> g k d h c", g=G, h=HG, k=2)
        wo_v = w_o.rearrange("(o p) (g n) -> g p o n", p=P, g=G)
        x_v = x.rearrange("(c t p) i -> c t p i", t=4, p=P)

        block = ctx.enter_context(nc.Block())

        @block.sync
        def _(sp):
            sp.dma_start(m.ident[:, :], ident_in).then_inc(const_loaded, 16)
            sp.dma_start(wa_rows[:, 0:3, :], w_qa.rearrange("(o p) i -> p o i", p=P)).then_inc(wa_loaded, 16)
            sp.dma_start(wa_rows[:, 3, :], w_kva[0:C]).then_inc(wa_loaded, 16)
            sp.dma_start(wa_tail[0:DR], w_kva[C:C + DR]).then_inc(wa_loaded, 16)
            sp.dma_start(q_w, q_ln.rearrange("(k p) -> p k", p=P),
                         allow_slow_non_contiguous=True).then_inc(const_loaded, 16)
            sp.dma_start(kv_w, kv_ln.rearrange("(k p) -> p k", p=P),
                         allow_slow_non_contiguous=True).then_inc(const_loaded, 16)
            sp.dma_start(mask, mask_in).then_inc(wq_free, 16)
            sp.dma_start(m.cos[:, :, :], cos_in.rearrange("(t p) d -> p t d", p=P)).then_inc(wo_free, 16)
            sp.dma_start(m.sin[:, :, :], sin_in.rearrange("(t p) d -> p t d", p=P)).then_inc(cq_free, 16)
            sp.dma_start(m.y_dram.rearrange("t p d -> (t p) d"), x).then_inc(m.y_stored, 16)

        @block.gpsimd
        def _(pool):
            def load_x(c, t):
                pool.dma_start(x_in[:, t, :], x_v[chunk(c), t]).then_inc(x_loaded[t], 16)

            def load_wq_rows(g):
                pool.dma_start(nope, wqb_v[g, 0:DN]).then_inc(nope_loaded, 16)
                for e in range(2):
                    pool.dma_start(pe_rows[DR * e:DR * e + DR], wpe_v[g, e, DN:DQ]).then_inc(pe_loaded, 16)

            def load_kv(g, k):
                pool.dma_start(kv[:, :, k, :], kvb_v[g, k]).then_inc(kv_loaded[k], 16)

            def load_wo_rows(g):
                pool.dma_start(wo_rows, wo_v[g]).then_inc(wor_loaded, 16)

            def turn(c, more):
                for t in range(4):
                    if more or t == 0:
                        pool.wait_ge(x_turned, c * 4 + t + 1)
                        load_x(c + 1 if more else 0, t)
                    b = t % 2
                    pool.wait_ge(eps_added, c * 4 + t + 1)
                    nc.gpsimd.tensor_tensor(rstd[:, 2 * b:2 * b + 2], safe[:, 2 * b:2 * b + 2], minus_half,
                                            ALU.pow).then_inc(rstd_done, 1)
                    if t == 1 and more:
                        pool.wait_ge(filled, c * FILLS + KR)
                        load_kv(c + 1, 0)
                    if t == 2 and more:
                        pool.wait_ge(filled, c * FILLS + WQ_SPLITS)
                        load_wq_rows(c + 1)
                    if t == 3 and more:
                        pool.wait_ge(filled, c * FILLS + WQ_SPLITS + HG)
                        load_wo_rows(c + 1)
                if more:
                    pool.wait_ge(filled, c * FILLS + FILLS)
                    load_kv(c + 1, 1)

            for t in range(4):
                load_x(0, t)
            load_kv(0, 0)
            load_wq_rows(0)
            load_wo_rows(0)
            load_kv(0, 1)
            with pool.Fori(0, NCH - 1) as c:
                turn(c, True)
            turn(NCH - 1, False)

        @block.tensor
        def _(pe):
            pe.wait_ge(const_loaded, 16 * 3)
            pe.wait_ge(wa_loaded, 48)
            for k in range(KH):
                for o in range(4):
                    pe.transpose(m.bank[k][:, o * P:o * P + P], wa_rows[:, o, k * P:k * P + P], m.ident[:, :])
            for k in range(KH):
                mm = pe.transpose(m.bank[4][:, k * DR:k * DR + DR], wa_tail[0:DR, k * P:k * P + P],
                                  m.ident[0:DR, 0:DR])
            mm.then_inc(wa_turned, 1)
            pe.wait_ge(wa_copied, KH + 1)

            def turn_x(c, t):
                if c is None:
                    pe.wait_ge(x_loaded[0], 16)
                else:
                    pe.wait_ge(x_loaded[t % 4], c * 16 + (16 if t < 4 else 32))
                    pe.wait_ge(xt_copied, c * 4 + t)
                for k in range(KH):
                    mm = pe.transpose(X[:, k * P:k * P + P], x_in[:, t % 4, k * P:k * P + P], m.ident[:, :])
                mm.then_inc(x_turned, 1)

            turn_x(None, 0)
            with pe.Fori(0, NCH) as c:

                def project(t):
                    pe.wait_ge(xt_copied, c * 4 + t + 1)
                    if t >= 2:
                        pe.wait_ge(cn_done, c * 4 + t - 1)
                    for k in range(KH):
                        pe.matmul(PROJ[t % 2], x_t[t % 2][:, k * P:k * P + P], wa_t[:, k, 0:QLR + C],
                                  start=(k == 0), stop=(k == KH - 1))
                    if t:
                        pe.wait_ge(rope_parts, c * 12 + 3 * t)
                    pe.wait_ge(tok_lo, TOK + c * TOK + 3 * max(t - 1, 0))
                    for k in range(KH):
                        mm = pe.matmul(KP, x_t[t % 2][:, k * P:k * P + P], wa_t[:, k, QLR + C:WA],
                                       start=(k == 0), stop=(k == KH - 1))
                    mm.then_inc(proj_ready, 1)

                def turn_results(t):
                    pe.wait_ge(tok_lo, TOK + c * TOK + 3 * t)
                    pe.wait_ge(cqn_done, c * 4 + t + 1)
                    for k in range(KR):
                        pe.transpose(TR[:, k * P:k * P + P], cq_n[t % 2][:, k * P:k * P + P], m.ident[:, :])
                    pe.wait_ge(cn_done, c * 4 + t + 1)
                    pe.transpose(TR[:, QLR:QLR + C], c_n[t % 2], m.ident[:, :])
                    pe.wait_ge(krot_done, c * 8 + 2 * t + 2)
                    if t < 3:
                        pe.wait_ge(rope_parts, c * 12 + 3 * t + 6)
                    pe.transpose(KT, k_rot[t % 2], m.ident[:, :]).then_inc(turned, 1)

                def fill(n):
                    kind, k = fills[n]
                    if n < 3:
                        pe.wait_ge(split_lo, c * SPLITS + split_of[last_in_bank(n)] + 1)
                    else:
                        if fills[n - 3][0] == "turn":
                            pe.wait_ge(wot_copied, c * HG + fills[n - 3][1] + 1)
                        else:
                            pe.wait_ge(split_lo, SPLITS + c * SPLITS + split_of[n - 3] + 1)
                    out = fill_bank(n)
                    if kind == "nope":
                        if k == 0:
                            pe.wait_ge(nope_loaded, c * 16 + 16)
                            pe.wait_ge(kv_loaded[0], c * 16 + 16)
                        for h in range(HG):
                            mm = pe.matmul(out[:, h * C:h * C + C], nope[:, h, k * P:k * P + P],
                                           kv[:, h, 0, :], start=True, stop=True)
                    elif kind == "pe":
                        if k == 0:
                            pe.wait_ge(pe_loaded, c * 32 + 32)
                        for a in range(PAIRS):
                            mm = pe.transpose(out[:, a * P:a * P + P], pe_rows[:, a, k * P:k * P + P],
                                              m.ident[:, :])
                    elif kind == "turn":
                        if k == 0:
                            pe.wait_ge(wor_loaded, c * 16 + 16)
                        for o in range(KH):
                            mm = pe.transpose(out[:, o * P:o * P + P], wo_rows[:, o, k * DV:k * DV + DV],
                                              m.ident[:, :])
                    else:
                        if k == 0:
                            pe.wait_ge(kv_loaded[1], c * 16 + 16)
                        pe.wait_ge(wot_copied, c * HG + k + 1)
                        mm = pe.matmul(out, kv[:, k, 1, :], wo_t[:, k, :], start=True, stop=True)
                    mm.then_inc(filled, 1)

                for t in range(4):
                    project(t)
                    turn_x(c, t + 1)
                    for n in beside[t]:
                        fill(n)
                    if t:
                        turn_results(t - 1)
                for n in at_end:
                    fill(n)
                turn_results(3)
            pe.wait_ge(xt_copied, NCH * 4 + 1)
            pe.wait_ge(tok_lo, TOK * (NCH + 1))
            pe.wait_ge(split_lo, SPLITS * (NCH + 1))

        def token_places(c, t):
            yield (TR[:, 0:QLR].rearrange("p (k n) -> p k n", k=KR), lambda a: m.cq[:, a, :, t * P:t * P + P], None)
            yield TR[:, QLR:QLR + C], lambda a: m.key_c[:, a, bass.ds(chunk(c) * 512 + t * P, P)], kv_w
            yield KT, lambda a: m.key_pe[:, a, bass.ds(chunk(c) * 512 + t * P, P)], None

        @block.scalar
        def _(act):
            act.wait_ge(wa_turned, 1)
            for k in range(KH):
                nc.scalar.copy(wa_t[:, k, 0:QLR + C], m.bank[k]).then_inc(wa_copied, 1)
            nc.scalar.copy(wa_t[:, :, QLR + C:WA], m.bank[4][:, 0:KH * DR].rearrange("p (k n) -> p k n", k=KH)
                           ).then_inc(wa_copied, 1)
            act.wait_ge(consts_made, 4)

            def copy_x(c, t):
                act.wait_ge(x_turned, 1 if c is None else c * 4 + t + 1)
                nc.scalar.copy(x_t[t % 2], X).then_inc(xt_copied, 1)

            copy_x(None, 0)
            with act.Fori(0, NCH) as c:
                def split(n):
                    act.wait_ge(filled, c * FILLS + n + 1)
                    if fills[n][0] == "turn":
                        nc.scalar.copy(wo_t[:, fills[n][1], :], fill_bank(n)).then_inc(wot_copied, 1)
                    else:
                        if n == 0:
                            act.wait_ge(wq_free, c * 16 + 16)
                        elif fills[n] == ("out", 0):
                            act.wait_ge(wo_free, c * 16 + 16)
                        src, dst, scale = split_places(n)
                        nc.scalar.activation(dst(0), src, ACT.Copy, scale=scale).then_inc(split_hi, 1)

                def hi(t):
                    if t == 0:
                        act.wait_ge(cq_free, c * 16 + 16)
                    act.wait_ge(turned, c * 4 + t + 1)
                    for src, dst, scale in token_places(c, t):
                        if scale is None:
                            nc.scalar.copy(dst(0), src).then_inc(tok_hi, 1)
                        else:
                            nc.scalar.activation(dst(0), src, ACT.Copy, scale=scale).then_inc(tok_hi, 1)

                for t in range(4):
                    b = t % 2
                    act.wait_ge(proj_ready, c * 4 + t + 1)
                    nc.scalar.activation(squares[:, 0:QLR], PROJ[b][:, 0:QLR], ACT.Square, scale=QLR ** -0.5,
                                         accum_out=means[:, 2 * b:2 * b + 1]).then_inc(squared, 1)
                    nc.scalar.activation(squares[:, QLR:QLR + C], PROJ[b][:, QLR:QLR + C], ACT.Square, scale=C ** -0.5,
                                         accum_out=means[:, 2 * b + 1:2 * b + 2]).then_inc(squared, 1)
                    copy_x(c, t + 1)
                    for n in beside[t]:
                        split(n)
                    act.wait_ge(rstd_done, c * 4 + t + 1)
                    nc.scalar.activation(cq_n[b], PROJ[b][:, 0:QLR], ACT.Copy,
                                         scale=rstd[:, 2 * b:2 * b + 1]).then_inc(cqn_done, 1)
                    if t:
                        hi(t - 1)
                    if t == 2:
                        act.wait_ge(split_lo, SPLITS + c * SPLITS + WQ_SPLITS)
                        act.dma_start(m.wq_dram[c], words(m.wq)).then_inc(wq_free, 16)
                for n in at_end:
                    split(n)
                act.wait_ge(split_lo, SPLITS + c * SPLITS + SPLITS)
                act.dma_start(m.wo_dram[c], words(m.wo)).then_inc(wo_free, 16)
                hi(3)
                act.wait_ge(tok_lo, TOK + c * TOK + TOK)
                act.dma_start(m.cq_dram[chunk(c)], words(m.cq)).then_inc(cq_free, 16)
            act.wait_ge(wq_free, 16 * (NCH + 1))

        @block.vector
        def _(dve):
            nc.vector.memset(minus_half, -0.5).then_inc(consts_made, 1)
            dve.wait_ge(const_loaded, 16 * 3)
            nc.vector.tensor_copy(m.ident16[:, :], m.ident[:, :]).then_inc(consts_made, 1)
            dve.wait_ge(wq_free, 16)
            nc.vector.tensor_copy(m.mask16[:, :], mask).then_inc(consts_made, 1)
            nc.vector.tensor_scalar(q_w, q_w, SCALE, None, ALU.mult).then_inc(consts_made, 1)
            dve.wait_ge(consts_made, 4)
            dve.wait_ge(wo_free, 16)
            dve.wait_ge(cq_free, 16)
            nc.vector.memset(m.small[:, 60:61], 0.0).then_inc(tok_lo, TOK)
            nc.vector.memset(m.small[:, 61:62], 0.0).then_inc(split_lo, SPLITS)
            with dve.Fori(0, NCH) as c:
                def split(n):
                    if fills[n][0] != "turn":
                        src, dst, scale = split_places(n)
                        dve.wait_ge(split_hi, c * SPLITS + split_of[n] + 1)
                        nc.vector.scalar_tensor_tensor(out=dst(1), in0=src, scalar=scale, in1=stored(dst(0)),
                                                       op0=ALU.mult, op1=ALU.subtract).then_inc(split_lo, 1)

                def lo(t):
                    for n, (src, dst, scale) in enumerate(token_places(c, t)):
                        dve.wait_ge(tok_hi, c * 12 + 3 * t + max(n, 1) + 1)
                        if scale is None:
                            nc.vector.tensor_tensor(dst(1), src, stored(dst(0)), ALU.subtract).then_inc(tok_lo, 1)
                        else:
                            nc.vector.scalar_tensor_tensor(out=dst(1), in0=src, scalar=scale, in1=stored(dst(0)),
                                                           op0=ALU.mult, op1=ALU.subtract).then_inc(tok_lo, 1)

                for t in range(4):
                    b = t % 2
                    tile = chunk(c) * 4 + t
                    dve.wait_ge(proj_ready, c * 4 + t + 1)
                    kp = KP.rearrange("p (a d) -> p a d", a=2)
                    cos_t = m.cos[:, bass.ds(tile, 1), :].broadcast_to([P, 2, HALF])
                    sin_t = m.sin[:, bass.ds(tile, 1), :]
                    tc = t_cos.rearrange("p (a d) -> p a d", a=2)
                    ts = t_sin.rearrange("p (a d) -> p a d", a=2)
                    nc.vector.tensor_tensor(tc, kp, cos_t, ALU.mult).then_inc(rope_parts, 1)
                    nc.vector.tensor_tensor(ts[:, 0:1], kp[:, 1:2], sin_t, ALU.mult).then_inc(rope_parts, 1)
                    nc.vector.tensor_tensor(ts[:, 1:2], kp[:, 0:1], sin_t, ALU.mult).then_inc(rope_parts, 1)
                    dve.wait_ge(rope_parts, c * 12 + 3 * t + 3)
                    kr = k_rot[b].rearrange("p (r a d) -> p r a d", r=2, a=2)
                    for a, op in ((0, ALU.subtract), (1, ALU.add)):
                        nc.vector.tensor_tensor(
                            kr[:, :, a, :], tc[:, a:a + 1, :].broadcast_to([P, 2, HALF]),
                            ts[:, a:a + 1, :].broadcast_to([P, 2, HALF]), op).then_inc(krot_done, 1)
                    dve.wait_ge(squared, c * 8 + 2 * t + 2)
                    nc.vector.tensor_scalar(safe[:, 2 * b:2 * b + 2], means[:, 2 * b:2 * b + 2], RMS_EPS, None,
                                            ALU.add).then_inc(eps_added, 1)
                    for n in beside[t]:
                        split(n)
                    dve.wait_ge(cqn_done, c * 4 + t + 1)
                    nc.vector.tensor_scalar(c_n[b], PROJ[b][:, QLR:QLR + C], rstd[:, 2 * b + 1:2 * b + 2],
                                            None, ALU.mult).then_inc(cn_done, 1)
                    dve.wait_ge(cn_done, c * 4 + t + 1)
                    v_hi = m.val[:, 0, bass.ds(tile, 1), :]
                    v_lo = m.val[:, 1, bass.ds(tile, 1), :]
                    cn3 = c_n[b].rearrange("p (a d) -> p a d", a=1)
                    nc.vector.tensor_copy(v_hi, cn3).then_inc(val_hi, 1)
                    dve.wait_ge(val_hi, c * 4 + t + 1)
                    nc.vector.tensor_tensor(v_lo, cn3, stored(v_hi), ALU.subtract)
                    if t:
                        lo(t - 1)
                for n in at_end:
                    split(n)
                lo(3)


Y_FIRST = NT - 5


def ffn_rows(m):
    return m.pool[:, 0:KH * HID].rearrange("p (o i) -> p o i", o=KH)


def all_sums(m):
    return m.pool[:, KH * HID:(KH + NT) * HID].rearrange("p (t d) -> p t d", t=NT)


def attention_phase(nc, m, w_ffn, scale_w):
    with ExitStack() as ctx:
        def sb(name, shape, dt=F32):
            return ctx.enter_context(nc.sbuf_tensor(name, shape, dt))

        def sem(name):
            return ctx.enter_context(nc.semaphore(name))

        even = m.pool[:, 0:HG * (NT - 1) * P].rearrange("p (h k) -> p h k", h=HG)
        odd = m.pool[:, HG * (NT - 1) * P:].rearrange("p (h k) -> p h k", h=HG)
        probs = [even, odd]
        q_c = sb("q_c", [P, 2, HG, 512], F32R)
        q_pe = sb("q_pe", [P, HG, 512], F32R)
        turned_p = sb("turned_p", [P, 2, 2, 512], F32R)
        o_t = sb("o_t", [P, 2, 512], F32R)
        y = sb("y", [P, 2, HID])
        rot_cos = sb("rot_cos", [P, HG * DR])
        rot_sin = sb("rot_sin", [P, HG * DR])
        rot = sb("rot", [P, HG * P])
        half_max = m.small[:, 20:22]
        neg_max = m.small[:, 24:24 + HG]
        part_sum = m.small[:, 28:28 + 4 * HG]
        row_sum = m.small[:, 44:44 + HG]
        inv_sum = m.small[:, 48:48 + HG]
        TURN, OUT, MISC = [m.bank[4], m.bank[5]], m.bank[6], m.bank[7]

        wq_loaded = sem("wq_loaded")
        wo_loaded = sem("wo_loaded")
        cq_loaded = sem("cq_loaded")
        y_loaded = [sem(f"y_loaded{n}") for n in range(2)]
        y_stored = m.y_stored
        y_added = sem("y_added")
        scores_ready = sem("scores_ready")
        half_max_done = sem("half_max_done")
        max_done = sem("max_done")
        exp_done = sem("exp_done")
        sum_done = sem("sum_done")
        inv_done = sem("inv_done")
        norm_done = sem("norm_done")
        p_turned = sem("p_turned")
        p_hi = sem("p_hi")
        p_lo = sem("p_lo")
        pv_done = sem("pv_done")
        o_hi = sem("o_hi")
        o_lo = sem("o_lo")
        misc_ready = sem("misc_ready")
        q_hi = sem("q_hi")
        q_lo = sem("q_lo")
        rope_cos = sem("rope_cos")
        rope_sum = sem("rope_sum")
        rope_hi = sem("rope_hi")
        rope_lo = sem("rope_lo")
        qpe_done = sem("qpe_done")

        def banks(i):
            return (i + 4) // 4

        def width(i):
            return (i + 1) * P

        def place(i, h):
            return h * banks(i) % 4

        def bank_of(i, h, c):
            return (place(i, h) + c // 512) % 4

        def columns(i, h, c0, c1):
            at = bank_of(i, h, c0) * 512
            return m.rows[:, at:at + c1 - c0]

        def halves(i, h):
            w = width(i)
            cut = 512 if place(i, h) == 3 else 1024
            return [(0, w)] if banks(i) <= 2 else [(0, cut), (cut, w)]

        def parts(i):
            w = width(i)
            return [(0, w)] if banks(i) <= 2 else [(c, min(c + 512, w)) for c in range(0, w, 512)]

        def score_count(i, h, b):
            return 4 * sum(banks(n) for n in range(i)) + h * banks(i) + b + 1

        def part_count(i, h, a):
            return 4 * sum(len(parts(n)) for n in range(i)) + h * len(parts(i)) + a + 1

        def two_part_count(i, h):
            return 4 * sum(len(parts(n)) > 1 for n in range(i)) + (h + 1)

        def head_count(i, h):
            return 4 * i + h + 1

        def key_count(i, j):
            return i * (i + 1) // 2 + j + 1

        SCORES, PARTS, HEADS, KEYS = score_count(NT, 0, -1), part_count(NT, 0, -1), 4 * NT, key_count(NT, -1)
        TWO = two_part_count(NT, -1)

        def quarter(i, h):
            n = i + 1
            return range(h * n // 4, (h + 1) * n // 4)

        def plan():
            for i in range(NT):
                for h in range(HG):
                    yield ("scores", i, h)
                    if h == 0 and i >= 1:
                        yield ("turn_probs", i - 1, 0)
                    if h == 0 and i >= 2:
                        yield ("y", i - 2)
                    if h == (0 if i < 2 else 1) and i + 1 < NT:
                        yield ("pe", i + 1)
                    if h == (1 if i < 2 else 2) and i + 1 < NT:
                        yield ("round_pe", i + 1)
                    if h == 3 and i + 1 < NT:
                        yield ("turn_pe", i + 1)
                    if i >= 1:
                        for j in quarter(i - 1, h):
                            yield ("work_off", i - 1, j)
                    yield ("normalise", i, h)
                    if i % 4 == 3 and i < NT - 1:
                        yield ("q", i // 4 + 1, h)
            between = {0: ("y", NT - 2), 2: ("q", NCH, 1), 4: ("q", NCH, 2), 6: ("q", NCH, 3),
                       8: ("pe", NT), 10: ("round_pe", NT), 11: ("turn_pe", NT)}
            yield ("q", NCH, 0)
            yield ("turn_probs", NT - 1, 0)
            for j in range(NT):
                yield ("work_off", NT - 1, j)
                if j in between:
                    yield between[j]
            yield ("y", NT - 1)

        START = [("pe", 0)] + [("q", 0, h) for h in range(HG)] + [("turn_pe", 0)]
        START_ALL = START[:3] + [("round_pe", 0)] + START[3:]
        uses = [u for u in plan() if u[0] in ("q", "pe", "turn_pe", "y")]
        use = {u: n for n, u in enumerate(uses)}
        USES = len(uses)

        def made(g, u):
            return START.index(u) + 1 if g is None else g * USES + len(START) + use[u] + 1

        def q_bank(g, h):
            return m.bank[h] if g is None else MISC

        def number(g, per_group, n):
            return n if g is None else g * per_group + n

        block = ctx.enter_context(nc.Block())

        @block.sync
        def _(sp):
            def load_cq(c, t0, t1):
                sp.dma_start(stored(m.cq[:, :, :, t0 * P:t1 * P].rearrange("p a k n -> p (a k) n")),
                             m.cq_dram[c].rearrange("p (a n) -> p a n", n=512)[:, :, t0 * P:t1 * P]
                             ).then_inc(cq_loaded, 16)

            def load_y(i):
                sp.dma_start(y[:, i % 2, :], m.y_dram[i]).then_inc(y_loaded[i % 2], 16)

            def store_y(g, i):
                sp.wait_ge(y_added, NT + g * NT + i + 1)
                sp.dma_start(m.y_dram[i], y[:, i % 2, :]).then_inc(y_stored, 16)

            sp.wait_ge(m.wo_free, 16 * (NCH + 1))
            sp.wait_ge(m.cq_free, 16 * (NCH + 1))
            with sp.Fori(0, G) as g:
                sp.dma_start(words(m.wo), m.wo_dram[(g + G - 1) % G]
                             ).then_inc(wo_loaded, 16)
                for i in range(NT):
                    if i == 1:
                        sp.wait_ge(y_stored, g * (16 * NT) + 16)
                    if i >= 3:
                        sp.wait_ge(y_stored, g * (16 * NT) + 16 * (i - 1))
                    if i >= 1:
                        load_y(i - 1)
                    if i >= 2:
                        store_y(g, i - 2)
                    if i % 4 in (1, 2):
                        sp.wait_ge(misc_ready, made(g, ("pe", i + 1)))
                        load_cq((i // 4 + 1) % NCH, *((0, 3) if i % 4 == 1 else (3, 4)))
                sp.wait_ge(y_stored, g * (16 * NT) + 16 * (NT - 1))
                load_y(NT - 1)
                store_y(g, NT - 2)
                store_y(g, NT - 1)
            sp.wait_ge(y_stored, 16 * (NT * G + 1))
            sp.wait_ge(cq_loaded, 32 * NCH * G)

        @block.tensor
        def _(pe):
            def wait_read(g, u):
                if u[0] == "q":
                    pe.wait_ge(q_lo, number(g, NCH * HG, u[1] * HG + u[2] + 1))
                elif u[0] == "pe":
                    pe.wait_ge(rope_cos, number(g, 3 * NT, 3 * u[1] + 3))
                elif u[0] == "turn_pe":
                    pe.wait_ge(qpe_done, number(g, NT, u[1] + 1))
                else:
                    pe.wait_ge(y_added, NT + number(g, NT, u[1] + 1))

            def shared(g, u):
                if g is None:
                    if u[0] == "turn_pe":
                        wait_read(g, ("pe", 0))
                elif use[u] == 0:
                    pe.wait_ge(y_added, g * NT + NT)
                else:
                    wait_read(g, uses[use[u] - 1])

            def project_q(g, c, h):
                shared(g, ("q", c, h))
                if g is not None and h == 0:
                    pe.wait_ge(cq_loaded, g * (32 * NCH) + 32 * c)
                    if c == NCH:
                        pe.wait_ge(wq_loaded, g * 16 + 16)
                n = 0
                for k in range(KR):
                    for a, b in ((0, 0), (1, 0), (0, 1)):
                        mm = pe.matmul(q_bank(g, h), m.wq[:, a, k, h * C:h * C + C], m.cq[:, b, k, :],
                                       start=(n == 0), stop=(n == 3 * KR - 1))
                        n += 1
                mm.then_inc(misc_ready, 1)

            def project_pe(g, t):
                shared(g, ("pe", t))
                n = 0
                for k in range(KR):
                    for a, b in ((0, 0), (1, 0), (0, 1)):
                        mm = pe.matmul(MISC[:, 0:HG * DR], m.cq[:, a, k, t % 4 * P:t % 4 * P + P],
                                       m.wq[:, b, k, HG * C:WCOL], start=(n == 0), stop=(n == 3 * KR - 1))
                        n += 1
                mm.then_inc(misc_ready, 1)

            def turn_pe(g, t):
                shared(g, ("turn_pe", t))
                pe.wait_ge(rope_lo, number(g, NT, t + 1))
                for h in range(HG):
                    mm = pe.transpose(MISC[:, h * P:h * P + P], rot[:, h * P:h * P + P], m.ident[:, :])
                mm.then_inc(misc_ready, 1)

            project_pe(None, 0)
            for h in range(HG):
                project_q(None, 0, h)
            turn_pe(None, 0)
            wait_read(None, START[-1])
            with pe.Fori(0, G) as g:
                def read_before(i, h, b):
                    bank = bank_of(i, h, 512 * b)
                    for n in range(4 * i + h - 1, -1, -1):
                        pi, ph = n // 4, n % 4
                        at = (bank - place(pi, ph)) % 4
                        if at < banks(pi):
                            return part_count(pi, ph, at if len(parts(pi)) > 1 else 0)
                    return 0

                def scores(i, h):
                    t = i % 4 * P
                    if i % 4 == 0:
                        pe.wait_ge(q_lo, g * (NCH * HG) + (i // 4) * HG + h + 1)
                    if h == 0:
                        pe.wait_ge(qpe_done, g * NT + i + 1)
                    for b in range(banks(i)):
                        before = read_before(i, h, b)
                        if before:
                            pe.wait_ge(exp_done, g * PARTS + before)
                        k0 = b * 512
                        n_k = min(512, width(i) - k0)
                        diagonal = b == banks(i) - 1
                        out = m.bank[bank_of(i, h, k0)]
                        row = out[:, 0:n_k]
                        terms = [(q_c[:, 0, h, t:t + P], m.key_c[:, 0, k0:k0 + n_k]),
                                 (q_c[:, 0, h, t:t + P], m.key_c[:, 1, k0:k0 + n_k]),
                                 (q_c[:, 1, h, t:t + P], m.key_c[:, 0, k0:k0 + n_k]),
                                 (q_pe[:, h, t:t + P], m.key_pe[:, 0, k0:k0 + n_k]),
                                 (q_pe[:, h, t:t + P], m.key_pe[:, 1, k0:k0 + n_k])]
                        for x, (q, k) in enumerate(terms):
                            mm = pe.matmul(row, q, k, start=(x == 0), stop=(x == 4 and not diagonal))
                        if diagonal:
                            mm = pe.matmul(row[:, n_k - P:n_k], m.ident16[:, :], m.mask16[:, :],
                                           start=False, stop=True)
                        mm.then_inc(scores_ready, 1)

                def turn_probs(i, j):
                    if j == 0:
                        pe.wait_ge(norm_done, g * HEADS + head_count(i, HG - 1))
                    n = key_count(i, j)
                    if n > 2:
                        pe.wait_ge(p_lo, g * KEYS + n - 2)
                    for h in range(HG):
                        mm = pe.transpose(TURN[n % 2][:, h * P:h * P + P], probs[i % 2][:, h, j * P:j * P + P],
                                          m.ident[:, :])
                    mm.then_inc(p_turned, 1)

                def values_hi(i, j):
                    if j == 0 and i > 0:
                        pe.wait_ge(o_lo, g * NT + i)
                    n = key_count(i, j)
                    pe.wait_ge(p_hi, g * KEYS + n)
                    pe.matmul(OUT, m.val[:, 0, j, :], turned_p[:, n % 2, 0, :], start=(j == 0), stop=False)
                    pe.matmul(OUT, m.val[:, 1, j, :], turned_p[:, n % 2, 0, :], start=False, stop=False)

                def values_lo(i, j):
                    n = key_count(i, j)
                    pe.wait_ge(p_lo, g * KEYS + n)
                    pe.matmul(OUT, m.val[:, 0, j, :], turned_p[:, n % 2, 1, :], start=False,
                              stop=(j == i)).then_inc(pv_done, 1)

                def work_off(i, j):
                    if j < i:
                        turn_probs(i, j + 1)
                    values_hi(i, j)
                    if j >= 1:
                        values_lo(i, j - 1)
                    if j == i:
                        values_lo(i, j)

                def project_out(i):
                    shared(g, ("y", i))
                    if i == 0:
                        pe.wait_ge(wo_loaded, g * 16 + 16)
                    pe.wait_ge(o_lo, g * NT + i + 1)
                    n = 0
                    for h in range(HG):
                        for a, b in ((0, 0), (0, 1), (1, 0)):
                            mm = pe.matmul(MISC, o_t[:, a, h * P:h * P + P], m.wo[:, b, h, :],
                                           start=(n == 0), stop=(n == 3 * HG - 1))
                            n += 1
                    mm.then_inc(misc_ready, 1)

                for what, *at in plan():
                    if what == "scores":
                        scores(*at)
                    elif what == "turn_probs":
                        turn_probs(*at)
                    elif what == "work_off":
                        work_off(*at)
                    elif what == "q":
                        project_q(g, *at)
                    elif what == "pe":
                        project_pe(g, *at)
                    elif what == "turn_pe":
                        turn_pe(g, *at)
                    elif what == "y":
                        project_out(*at)

        @block.scalar
        def _(act):
            def other(g, u):
                if u[0] == "q":
                    act.wait_ge(misc_ready, made(g, u))
                    nc.scalar.copy(q_c[:, 0, u[2], :], q_bank(g, u[2])).then_inc(q_hi, 1)
                elif u[0] == "round_pe":
                    act.wait_ge(rope_sum, number(g, 2 * NT, 2 * u[1] + 2))
                    nc.scalar.copy(rot[:, :].bitcast(F32R).rearrange("p (h a d) -> p h a d", h=HG, a=2)[:, :, 0, :],
                                   rot_cos[:, :].rearrange("p (h d) -> p h d", h=HG)).then_inc(rope_hi, 1)
                elif u[0] == "turn_pe":
                    t = u[1] % 4 * P
                    act.wait_ge(misc_ready, made(g, u))
                    nc.scalar.copy(q_pe[:, :, t:t + P], MISC.rearrange("p (h n) -> p h n", h=HG)).then_inc(qpe_done, 1)

            for u in START_ALL:
                other(None, u)
            with act.Fori(0, G) as g:
                def hi(i, j):
                    n = key_count(i, j)
                    act.wait_ge(p_turned, g * KEYS + n)
                    nc.scalar.copy(turned_p[:, n % 2, 0, :], TURN[n % 2]).then_inc(p_hi, 1)

                def exp(i, h, a):
                    c0, c1 = parts(i)[a]
                    act.wait_ge(max_done, g * HEADS + head_count(i, h))
                    row = columns(i, h, c0, c1)
                    nc.scalar.activation(probs[i % 2][:, h, c0:c1], row, ACT.Exp, bias=neg_max[:, h:h + 1],
                                         accum_out=part_sum[:, 4 * h + a:4 * h + a + 1]).then_inc(exp_done, 1)

                due = []
                first_of_head = [(i, quarter(i, h)[0]) for i in range(NT - 1) for h in range(HG)
                                 if len(quarter(i, h)) > 1 and banks(i + 1) == 4]
                for what, *at in plan():
                    if what == "scores":
                        due = [(*at, a) for a in range(len(parts(at[0])))]
                    elif what == "turn_probs":
                        hi(*at)
                    elif what == "work_off":
                        i, j = at
                        if j < i:
                            hi(i, j + 1)
                        if due and (i, j) not in first_of_head:
                            exp(*due.pop(0))
                        if j == i:
                            act.wait_ge(pv_done, g * KEYS + key_count(i, i))
                            nc.scalar.copy(o_t[:, 0, :], OUT).then_inc(o_hi, 1)
                    elif what == "normalise":
                        for x in due:
                            exp(*x)
                        due = []
                    else:
                        other(g, (what, *at))

        @block.gpsimd
        def _(pool):
            hi = rot[:, :].rearrange("p (h a d) -> p h a d", h=HG, a=2)[:, :, 0, :]
            lo = rot[:, :].rearrange("p (h a d) -> p h a d", h=HG, a=2)[:, :, 1, :]
            ca = rot_cos[:, :].rearrange("p (h a d) -> p h a d", h=HG, a=2)
            sa = rot_sin[:, :].rearrange("p (h a d) -> p h a d", h=HG, a=2)
            def rotate(n):
                pool.wait_ge(rope_cos, n * 3 + 3)
                nc.gpsimd.tensor_tensor(ca[:, :, 0, :], ca[:, :, 0, :], sa[:, :, 0, :], ALU.subtract
                                        ).then_inc(rope_sum, 1)
                nc.gpsimd.tensor_tensor(ca[:, :, 1, :], ca[:, :, 1, :], sa[:, :, 1, :], ALU.add
                                        ).then_inc(rope_sum, 1)
                pool.wait_ge(rope_hi, n + 1)
                nc.gpsimd.tensor_tensor(lo, rot_cos[:, :].rearrange("p (h d) -> p h d", h=HG), hi,
                                        ALU.subtract).then_inc(rope_lo, 1)

            rotate(0)
            with pool.Fori(0, G) as g:
                with pool.Fori(1, NT) as t:
                    rotate(g * NT + t)
                pool.wait_ge(misc_ready, made(g, ("pe", NT - 1)))
                pool.dma_start(words(m.wq), m.wq_dram[g]).then_inc(wq_loaded, 16)
                rotate(g * NT + NT)
            pool.wait_ge(wq_loaded, 16 * G)
            pool.wait_ge(misc_ready, len(START) + (G - 1) * USES + use[("pe", NT)] + 1)
            pool.dma_start(ffn_rows(m), w_ffn.rearrange("(o p) i -> p o i", p=P)).then_inc(m.ffn_w_loaded, 16)
            pool.dma_start(m.small[:, 0:4], scale_w.rearrange("(o p) -> p o", p=P),
                           allow_slow_non_contiguous=True).then_inc(m.ffn_w_loaded, 16)
            pool.wait_ge(y_stored, 16 * ((G - 1) * NT + Y_FIRST + 1))
            pool.dma_start(all_sums(m)[:, 0:Y_FIRST, :], m.y_dram.rearrange("t p d -> p t d")[:, 0:Y_FIRST, :]
                           ).then_inc(m.y_first_loaded, 16)

        @block.vector
        def _(dve):
            def other(g, u):
                if u[0] == "q":
                    _, c, h = u
                    dve.wait_ge(q_hi, number(g, NCH * HG, c * HG + h + 1))
                    nc.vector.tensor_tensor(q_c[:, 1, h, :], q_bank(g, h), stored(q_c[:, 0, h, :]), ALU.subtract
                                            ).then_inc(q_lo, 1)
                elif u[0] == "pe":
                    t = u[1] % NT
                    dve.wait_ge(misc_ready, made(g, u))
                    q = MISC[:, 0:HG * DR].rearrange("p (h a d) -> p h a d", h=HG, a=2)
                    ca = rot_cos[:, :].rearrange("p (h d) -> p h d", d=HALF)
                    sa = rot_sin[:, :].rearrange("p (h a d) -> p h a d", h=HG, a=2)
                    cos_t = m.cos[:, t:t + 1, :].broadcast_to([P, 2 * HG, HALF])
                    sin_t = m.sin[:, t:t + 1, :].broadcast_to([P, HG, HALF])
                    nc.vector.tensor_tensor(ca, MISC[:, 0:HG * DR].rearrange("p (h d) -> p h d", d=HALF), cos_t,
                                            ALU.mult).then_inc(rope_cos, 1)
                    nc.vector.tensor_tensor(sa[:, :, 0, :], q[:, :, 1, :], sin_t, ALU.mult).then_inc(rope_cos, 1)
                    nc.vector.tensor_tensor(sa[:, :, 1, :], q[:, :, 0, :], sin_t, ALU.mult).then_inc(rope_cos, 1)
                elif u[0] == "y":
                    i = u[1]
                    dve.wait_ge(misc_ready, made(g, u))
                    dve.wait_ge(y_loaded[i % 2], g * (8 * NT) + 16 * (i // 2 + 1))
                    nc.vector.tensor_tensor(y[:, i % 2, :], MISC, y[:, i % 2, :], ALU.add).then_inc(y_added, 1)

            nc.vector.memset(m.small[:, 60:61], 0.0).then_inc(y_added, NT)
            for u in START:
                other(None, u)
            with dve.Fori(0, G) as g:
                def lo(i, j):
                    n = key_count(i, j)
                    dve.wait_ge(p_hi, g * KEYS + n)
                    if n > 2:
                        dve.wait_ge(pv_done, g * KEYS + n - 2)
                    nc.vector.tensor_tensor(turned_p[:, n % 2, 1, :], TURN[n % 2], stored(turned_p[:, n % 2, 0, :]),
                                            ALU.subtract).then_inc(p_lo, 1)

                def maxima(i, h):
                    for a, (c0, c1) in enumerate(halves(i, h)):
                        dve.wait_ge(scores_ready, g * SCORES + score_count(i, h, (c1 - 1) // 512))
                        row = columns(i, h, c0, c1)
                        if banks(i) <= 2:
                            nc.vector.tensor_reduce(neg_max[:, h:h + 1], row, AX.X, ALU.max, negate=True
                                                    ).then_inc(max_done, 1)
                        else:
                            nc.vector.tensor_reduce(half_max[:, a:a + 1], row, AX.X, ALU.max
                                                    ).then_inc(half_max_done, 1)
                    if banks(i) > 2:
                        dve.wait_ge(half_max_done, g * (2 * TWO) + 2 * two_part_count(i, h))
                        nc.vector.tensor_reduce(neg_max[:, h:h + 1], half_max, AX.X, ALU.max, negate=True
                                                ).then_inc(max_done, 1)

                def normalise(i, h):
                    n_parts = len(parts(i))
                    dve.wait_ge(exp_done, g * PARTS + part_count(i, h, n_parts - 1))
                    total = part_sum[:, 4 * h:4 * h + 1]
                    if n_parts > 1:
                        total = row_sum[:, h:h + 1]
                        nc.vector.tensor_reduce(total, part_sum[:, 4 * h:4 * h + n_parts], AX.X, ALU.add
                                                ).then_inc(sum_done, 1)
                        dve.wait_ge(sum_done, g * TWO + two_part_count(i, h))
                    nc.vector.reciprocal(inv_sum[:, h:h + 1], total).then_inc(inv_done, 1)
                    dve.wait_ge(inv_done, g * HEADS + head_count(i, h))
                    p = probs[i % 2][:, h, 0:width(i)]
                    nc.vector.tensor_scalar(p, p, inv_sum[:, h:h + 1], None, ALU.mult).then_inc(norm_done, 1)

                for what, *at in plan():
                    if what == "scores":
                        maxima(*at)
                    elif what == "turn_probs":
                        lo(*at)
                    elif what == "work_off":
                        i, j = at
                        if j < i:
                            lo(i, j + 1)
                        else:
                            dve.wait_ge(o_hi, g * NT + i + 1)
                            nc.vector.tensor_tensor(o_t[:, 1, :], OUT, stored(o_t[:, 0, :]), ALU.subtract
                                                    ).then_inc(o_lo, 1)
                    elif what == "normalise":
                        normalise(*at)
                    else:
                        other(g, (what, *at))


def ffn_phase(nc, m, bias, out):
    with ExitStack() as ctx:
        def sem(name):
            return ctx.enter_context(nc.semaphore(name))

        at = 0

        def stage(n):
            nonlocal at
            at += n
            return m.pool[:, at - n:at]

        def sb(name, n):
            return ctx.enter_context(nc.sbuf_tensor(name, [P, n], F32))[:, :]

        stage((KH + NT) * HID)
        y_all = all_sums(m)
        w_rows = ffn_rows(m)
        w_s = stage(KH * HID).rearrange("p (o i) -> p o i", o=KH)
        w_t = sb("w_t", KH * HID).rearrange("p (k o) -> p k o", k=KH)
        bias_rows = sb("bias_rows", HID)
        x1 = [sb(f"x1_{b}", HID) for b in range(2)]
        x1b = [sb(f"x1b_{b}", HID) for b in range(2)]
        x1_t = [sb(f"x1t_{b}", HID) for b in range(2)]
        z = [sb(f"z_{b}", HID) for b in range(2)]
        o_out = [sb(f"o_out{b}", HID) for b in range(2)]
        w_scale = m.small[:, 0:4]
        minus_half = m.small[:, 4:5]
        spare = m.small[:, 5:6]
        epsilon = m.small[:, 6:7]
        stats = [m.small[:, 8 + 6 * b:14 + 6 * b] for b in range(4)]
        agg = [m.small[:, 32 + 2 * b:34 + 2 * b] for b in range(4)]
        safe = [m.small[:, 40 + b:41 + b] for b in range(4)]
        inv = [m.small[:, 44 + b:45 + b] for b in range(4)]

        w_loaded, y_first_loaded = m.ffn_w_loaded, m.y_first_loaded
        y_rest_loaded = sem("y_rest_loaded")
        w_scaled = sem("ffn_w_scaled")
        w_turned = sem("ffn_w_turned")
        w_copied = sem("ffn_w_copied")
        half_set = sem("half_set")
        bn_done = sem("bn_done")
        aggr_done = sem("aggr_done")
        ln_eps_added = sem("ln_eps_added")
        inv_ready = sem("inv_ready")
        x1_done = sem("x1_done")
        x1b_done = sem("x1b_done")
        x1_turned = sem("x1_turned")
        x1t_copied = sem("x1t_copied")
        lin_ready = sem("lin_ready")
        z_done = sem("z_done")
        AHEAD = 2
        out_done = sem("out_done")
        out_free = [sem(f"out_free{n}") for n in range(2)]

        block = ctx.enter_context(nc.Block())
        out_v = out.rearrange("(t p) d -> t p d", p=P)
        LOOPED = NT - 4

        def turns(eng, tile):
            with eng.Fori(0, LOOPED // 2) as n:
                tile(n * 2, 0, 3)
                tile(n * 2 + 1, 1, 3)
            for u in range(LOOPED, NT):
                tile(u, u % 2, min(3, NT - 1 - u))

        def y_number(u):
            return u * 2 + 3

        def z_number(u, after):
            return u * 2 + 4 if after == 3 else u + NT

        @block.sync
        def _(sp):
            y_v = m.y_dram.rearrange("t p d -> p t d")
            sp.dma_start(y_all[:, Y_FIRST:NT, :], y_v[:, Y_FIRST:NT, :]).then_inc(y_rest_loaded, 16)

        @block.gpsimd
        def _(pool):
            def invert(b, idx):
                pool.wait_ge(aggr_done, idx + 1)
                nc.gpsimd.tensor_tensor(safe[b], agg[b][:, 1:2], epsilon, ALU.add).then_inc(ln_eps_added, 1)
                pool.wait_ge(ln_eps_added, idx + 1)
                nc.gpsimd.tensor_tensor(inv[b], safe[b], minus_half, ALU.pow).then_inc(inv_ready, 1)

            def add_bias(u, b):
                pool.wait_ge(x1_done, u + 1)
                nc.gpsimd.tensor_tensor(x1b[b], x1[b], bias_rows, ALU.add).then_inc(x1b_done, 1)

            def tile(u, b, after):
                if after == 3:
                    invert(1 - b, y_number(u))
                invert(2 + b, z_number(u, after))
                if after >= 2:
                    pool.wait_ge(z_done, AHEAD + u + 1)
                    add_bias(u + 2, b)
                pool.wait_ge(out_done, u + 1)
                pool.dma_start(out_v[u], o_out[b]).then_inc(out_free[b], 16)

            pool.dma_start(bias_rows[:, 0:HID // 2], bias.rearrange("(a d) -> a d", a=1)[:, 0:HID // 2]
                           .broadcast_to([P, HID // 2])).then_inc(out_free[0], 16)
            pool.dma_start(bias_rows[:, HID // 2:HID], bias.rearrange("(a d) -> a d", a=1)[:, HID // 2:HID]
                           .broadcast_to([P, HID // 2])).then_inc(out_free[1], 16)
            pool.wait_ge(half_set, 3)
            invert(0, 0)
            invert(1, 1)
            for b in range(2):
                pool.wait_ge(out_free[b], 16)
            add_bias(0, 0)
            invert(0, 2)
            add_bias(1, 1)
            turns(pool, tile)
            for b in range(2):
                pool.wait_ge(out_free[b], 16 * (NT // 2 + 1))

        @block.tensor
        def _(pe):
            for o in range(KH):
                pe.wait_ge(w_scaled, o + 1)
                for k in range(KH):
                    mm = pe.transpose(m.bank[4 + k][:, o * P:o * P + P], w_s[:, o, k * P:k * P + P], m.ident[:, :])
                    if o == KH - 1:
                        mm.then_inc(w_turned, 1)

            def turn_x1(u, b):
                pe.wait_ge(x1_done, u + 1)
                for k in range(KH):
                    mm = pe.transpose(m.bank[b][:, k * P:k * P + P], x1[b][:, k * P:k * P + P], m.ident[:, :])
                mm.then_inc(x1_turned, 1)

            def linear(u, b, ks):
                if 0 in ks:
                    pe.wait_ge(x1t_copied, u + 1)
                    pe.wait_ge(z_done, AHEAD + u - 1)
                for k in ks:
                    mm = pe.matmul(m.bank[2 + b], x1_t[b][:, k * P:k * P + P], w_t[:, k, :],
                                   start=(k == 0), stop=(k == KH - 1))
                if KH - 1 in ks:
                    mm.then_inc(lin_ready, 1)

            def tile(u, b, after):
                linear(u, b, range(0, 2))
                if after:
                    turn_x1(u + 1, 1 - b)
                linear(u, b, range(2, KH))

            turn_x1(0, 0)
            pe.wait_ge(w_copied, KH)
            turns(pe, tile)

        @block.scalar
        def _(act):
            act.wait_ge(w_loaded, 32)
            for o in range(KH):
                nc.scalar.activation(w_s[:, o, :], w_rows[:, o, :], ACT.Copy, scale=w_scale[:, o:o + 1]
                                     ).then_inc(w_scaled, 1)
            for k in range(KH):
                act.wait_ge(w_turned, k + 1)
                nc.scalar.copy(w_t[:, k, :], m.bank[4 + k]).then_inc(w_copied, 1)

            def copy_x1(u, b):
                act.wait_ge(x1_turned, u + 1)
                nc.scalar.copy(x1_t[b], m.bank[b]).then_inc(x1t_copied, 1)

            def tile(u, b, after):
                if after:
                    copy_x1(u + 1, 1 - b)

            copy_x1(0, 0)
            turns(act, tile)

        @block.vector
        def _(dve):
            nc.vector.memset(minus_half, -0.5).then_inc(half_set, 1)

            nc.vector.memset(epsilon, LN_EPS).then_inc(half_set, 1)
            nc.vector.memset(m.small[:, 60:61], 0.0).then_inc(z_done, AHEAD)
            nc.vector.memset(m.small[:, 61:62], 0.0).then_inc(half_set, 1)

            def statistics(src, slot, number):
                nc.vector.bn_stats(stats[slot], src).then_inc(bn_done, 1)
                dve.wait_ge(bn_done, number + 1)
                nc.vector.memset(spare, 0.0)
                nc.vector.bn_aggr(agg[slot], stats[slot]).then_inc(aggr_done, 1)

            def y_tile(u):
                return y_all[:, bass.ds(u, 1), :].rearrange("p a d -> p (a d)")

            def apply(src, dst, slot, done):
                nc.vector.tensor_scalar(dst, src, agg[slot][:, 0:1], inv[slot], ALU.subtract, ALU.mult
                                        ).then_inc(done, 1)

            def tile(u, b, after):
                if after >= 2:
                    dve.wait_ge(x1_turned, u + 1)
                    dve.wait_ge(x1b_done, u + 1)
                    apply(y_tile(u + 2), x1[b], b, x1_done)
                if after == 3:
                    statistics(y_tile(u + 3), 1 - b, y_number(u))
                dve.wait_ge(lin_ready, u + 1)
                dve.wait_ge(x1b_done, u + 1)
                nc.vector.tensor_tensor(z[b], m.bank[2 + b], x1b[b], ALU.add).then_inc(z_done, 1)
                dve.wait_ge(z_done, AHEAD + u + 1)
                statistics(z[b], 2 + b, z_number(u, after))
                dve.wait_ge(out_free[b], (u - b) * 8 + 16)
                dve.wait_ge(inv_ready, z_number(u, after) + 1)
                apply(z[b], o_out[b], 2 + b, out_done)

            dve.wait_ge(y_first_loaded, 16)
            statistics(y_tile(0), 0, 0)
            statistics(y_tile(1), 1, 1)
            dve.wait_ge(inv_ready, 2)
            apply(y_tile(0), x1[0], 0, x1_done)
            apply(y_tile(1), x1[1], 1, x1_done)
            dve.wait_ge(x1_done, 2)
            statistics(y_tile(2), 0, 2)
            dve.wait_ge(y_rest_loaded, 16)
            dve.wait_ge(inv_ready, 3)
            turns(dve, tile)


def build(nc, x, w_qa, q_ln, w_qb, w_kva, kv_ln, w_kvb, w_o, ffn_w, ffn_scale, ffn_bias,
          ident_in, mask_in, cos_in, sin_in, out):
    with ExitStack() as ctx:
        m = Memory(nc, ctx)
        x2, out2 = x[0], out[0]
        prepare_phase(nc, m, x2, w_qa, w_kva, w_qb, w_kvb, w_o, q_ln, kv_ln, ident_in, mask_in, cos_in, sin_in)
        attention_phase(nc, m, ffn_w, ffn_scale)
        ffn_phase(nc, m, ffn_bias, out2)


_INS = ['L0_attn_hidden_states', 'L0_attn_w_qa', 'L0_attn_q_a_ln_w', 'L0_attn_w_qb', 'L0_attn_w_kva',
        'L0_attn_kv_a_ln_w', 'L0_attn_w_kvb', 'L0_attn_w_o', 'L0_ffn_weight', 'L0_ffn_scale_weight',
        'L0_ffn_bias']


def _constants():
    inv_freq = (1.0 / np.float32(10000.0) ** (np.arange(0, DR, 2, dtype=np.float32) / np.float32(DR))).astype(np.float32)
    angle = np.outer(np.arange(S, dtype=np.float32), inv_freq).astype(np.float32)
    return {
        "ident": np.eye(P, dtype=np.float32),
        "mask": np.triu(np.full((P, P), MASKED, np.float32), k=1),
        "cos": np.cos(angle).astype(np.float32),
        "sin": np.sin(angle).astype(np.float32),
    }


def kernel(**inputs):
    import numpy as _np
    import concourse.bacc as _bacc
    from concourse import mybir as _mybir
    from concourse.bass_utils import run_bass_kernel_spmd as _run

    nc = _bacc.Bacc("TRN2", target_bir_lowering=False, num_devices=1)
    arrays, args = {}, []
    named = {f"in_{n}": _np.ascontiguousarray(inputs[n]) for n in _INS}
    named.update({f"const_{n}": a for n, a in _constants().items()})
    for name, a in named.items():
        arrays[name] = a
        args.append(nc.dram_tensor(name, a.shape, _mybir.dt.from_np(a.dtype), kind="ExternalInput").ap())
    out = nc.dram_tensor("out_dram", (1, S, HID), _mybir.dt.float32, kind="ExternalOutput").ap()
    build(nc, *args, out)
    r = _run(nc, [arrays], core_ids=[0])
    return r.results[0]["out_dram"]
```
